# Optimizing a Trainium2 kernel written in Bass

```python
import numpy as np
import jax
import jax.numpy as jnp

def _softmax(x, axis=-1):
    return jax.nn.softmax(x, axis=axis)

def _gelu(x):
    return jax.nn.gelu(x, approximate=True)

def _silu(x):
    return jax.nn.silu(x)

def _sigmoid(x):
    return jax.nn.sigmoid(x)

def _layernorm(x, axis=-1, eps=1e-05):
    m = jnp.mean(x, axis=axis, keepdims=True)
    v = jnp.var(x, axis=axis, keepdims=True)
    return (x - m) / jnp.sqrt(v + eps)

def _scatter_add(tgt, idx, src, axis=0):
    return tgt.at[idx].add(src)

def _segment_sum(src, seg, n):
    return jax.ops.segment_sum(src, seg, n)
kernel_name = 'mk_prb_d1_jaxref_r8_132ffe'

def setup_inputs(seed: int=0):
    np.random.seed(seed)
    _w = jnp.asarray

    def _L0_attn_setup():
        import jax, jax.numpy as jnp
        import numpy as np
        import math
        N_HEAD = 16
        WINDOW = 64
        SINK = 4

        def _sliding_window_sink_mask(T, window, sink):
            i = jnp.arange(T)[:, None]
            j = jnp.arange(T)[None, :]
            causal_band = (j <= i) & (j >= i - (window - 1))
            sink_cols = (j < sink) & (j <= i)
            return causal_band | sink_cols
        key = jax.random.key(seed)
        ks = jax.random.split(key, 6)
        B, T, C, L = (2, 256, 256, 64)
        s = 0.02
        return {'x': jax.random.normal(ks[0], (B, T, C), jnp.float32), 'Wq': jax.random.normal(ks[1], (C, C), jnp.float32) * s, 'Wkv_down': jax.random.normal(ks[2], (L, C), jnp.float32) * s, 'Wk_up': jax.random.normal(ks[3], (C, L), jnp.float32) * s, 'Wv_up': jax.random.normal(ks[4], (C, L), jnp.float32) * s, 'Wo': jax.random.normal(ks[5], (C, C), jnp.float32) * s}
    _L0_attn_in = _L0_attn_setup()

    def _L0_ffn_setup():
        import jax, jax.numpy as jnp
        import numpy as np
        EPS = 1e-06
        Q_B = 128.0

        def layer_norm(x):
            mean = jnp.mean(x, axis=-1, keepdims=True)
            var = jnp.var(x, axis=-1, keepdims=True)
            return (x - mean) / jnp.sqrt(var + EPS)

        def absmax_quant(x):
            gamma = jnp.max(jnp.abs(x), axis=-1, keepdims=True)
            x_hat = jnp.clip(x * Q_B / gamma, -Q_B + EPS, Q_B - EPS)
            return x_hat * gamma / Q_B

        def ternarize_weights(w):
            gamma = jnp.mean(jnp.abs(w))
            return jnp.sign(jnp.round(w / (gamma + EPS))) * gamma

        def bitlinear(x, w):
            xn = layer_norm(x)
            x_hat = xn + jax.lax.stop_gradient(absmax_quant(xn) - xn)
            w_hat = w + jax.lax.stop_gradient(ternarize_weights(w) - w)
            return jnp.einsum('bsd,od->bso', x_hat, w_hat)
        key = jax.random.key(seed)
        k1, k2, k3 = jax.random.split(key, 3)
        B, S, D = (4, 256, 256)
        x = jax.random.normal(k1, (B, S, D), dtype=jnp.float32)
        w_fc = jax.random.normal(k2, (4 * D, D), dtype=jnp.float32) / np.sqrt(D)
        w_proj = jax.random.normal(k3, (D, 4 * D), dtype=jnp.float32) / np.sqrt(4 * D)
        return {'x': x, 'w_fc': w_fc, 'w_proj': w_proj}
    _L0_ffn_in = _L0_ffn_setup()
    _d = {'L0_attn_x': _L0_attn_in['x'], 'L0_attn_Wq': _L0_attn_in['Wq'], 'L0_attn_Wkv_down': _L0_attn_in['Wkv_down'], 'L0_attn_Wk_up': _L0_attn_in['Wk_up'], 'L0_attn_Wv_up': _L0_attn_in['Wv_up'], 'L0_attn_Wo': _L0_attn_in['Wo'], 'L0_ffn_w_fc': _L0_ffn_in['w_fc'], 'L0_ffn_w_proj': _L0_ffn_in['w_proj']}
    _x0 = _d['L0_attn_x']
    _d['L0_attn_x'] = jax.random.normal(jax.random.fold_in(jax.random.key(seed), 1), (4, 256, 256), dtype=_x0.dtype)
    del _x0
    return _d

def reference(L0_attn_x, L0_attn_Wq, L0_attn_Wkv_down, L0_attn_Wk_up, L0_attn_Wv_up, L0_attn_Wo, L0_ffn_w_fc, L0_ffn_w_proj):

    def _L0_attn_ref(x, Wq, Wkv_down, Wk_up, Wv_up, Wo):
        import jax, jax.numpy as jnp
        import numpy as np
        import math
        N_HEAD = 16
        WINDOW = 64
        SINK = 4

        def _sliding_window_sink_mask(T, window, sink):
            i = jnp.arange(T)[:, None]
            j = jnp.arange(T)[None, :]
            causal_band = (j <= i) & (j >= i - (window - 1))
            sink_cols = (j < sink) & (j <= i)
            return causal_band | sink_cols
        B, T, C = x.shape
        H = N_HEAD
        hd = C // H
        q = (x @ Wq.T).reshape(B, T, H, hd).transpose(0, 2, 1, 3)
        latent = x @ Wkv_down.T
        k = (latent @ Wk_up.T).reshape(B, T, H, hd).transpose(0, 2, 1, 3)
        v = (latent @ Wv_up.T).reshape(B, T, H, hd).transpose(0, 2, 1, 3)
        att = jnp.einsum('bhqd,bhkd->bhqk', q, k) / math.sqrt(hd)
        mask = _sliding_window_sink_mask(T, WINDOW, SINK)
        att = jnp.where(mask[None, None], att, -jnp.inf)
        att = jax.nn.softmax(att, axis=-1)
        y = jnp.einsum('bhqk,bhkd->bhqd', att, v)
        y = y.transpose(0, 2, 1, 3).reshape(B, T, C)
        return y @ Wo.T

    def _L0_ffn_ref(x, w_fc, w_proj):
        import jax, jax.numpy as jnp
        import numpy as np
        EPS = 1e-06
        Q_B = 128.0

        def layer_norm(x):
            mean = jnp.mean(x, axis=-1, keepdims=True)
            var = jnp.var(x, axis=-1, keepdims=True)
            return (x - mean) / jnp.sqrt(var + EPS)

        def absmax_quant(x):
            gamma = jnp.max(jnp.abs(x), axis=-1, keepdims=True)
            x_hat = jnp.clip(x * Q_B / gamma, -Q_B + EPS, Q_B - EPS)
            return x_hat * gamma / Q_B

        def ternarize_weights(w):
            gamma = jnp.mean(jnp.abs(w))
            return jnp.sign(jnp.round(w / (gamma + EPS))) * gamma

        def bitlinear(x, w):
            xn = layer_norm(x)
            x_hat = xn + jax.lax.stop_gradient(absmax_quant(xn) - xn)
            w_hat = w + jax.lax.stop_gradient(ternarize_weights(w) - w)
            return jnp.einsum('bsd,od->bso', x_hat, w_hat)
        h = bitlinear(x, w_fc)
        h = jax.nn.gelu(h, approximate=False)
        return bitlinear(h, w_proj)
    x = L0_attn_x
    xn = _layernorm(x, axis=-1)
    x = x + _L0_attn_ref(xn, L0_attn_Wq, L0_attn_Wkv_down, L0_attn_Wk_up, L0_attn_Wv_up, L0_attn_Wo) + _L0_ffn_ref(xn, L0_ffn_w_fc, L0_ffn_w_proj)
    return x

_drawn_inputs = setup_inputs


def setup_inputs(seed=0):
    import zlib

    import numpy as np

    out = dict(_drawn_inputs(seed))
    spreads = {}
    factors = {'L0_attn_Wq': 8.0,
     'L0_attn_Wkv_down': 8.0,
     'L0_attn_Wk_up': 8.0,
     'L0_attn_Wv_up': 8.0,
     'L0_attn_Wo': 8.0}
    for name, (base, spread) in spreads.items():
        noise = np.random.default_rng([zlib.crc32(name.encode()), seed]).standard_normal(out[name].shape)
        drawn = base * np.exp(spread * noise) if base else spread * noise
        out[name] = jnp.asarray(drawn.astype(out[name].dtype))
    for name, factor in factors.items():
        out[name] = (out[name] * factor).astype(out[name].dtype)
    return out
```

```python
import concourse.bass as bass
from concourse import mybir
from contextlib import ExitStack

B, T, C, L, H, F = 4, 256, 256, 64, 16, 1024
HD = C // H
P = 128
WINDOW, SINK = 64, 4
TT_ = T // P
CC = C // P
FC = F // P
G = 4
NT = H // G
BLK = 64
VW = HD + 1
QB = 128.0
LN_EPS, FFN_EPS = 1e-5, 1e-6
BIAS_ROWS = BLK + 2 * H + SINK
MASKED = -(2.0 ** 100)


def layer_kernel(nc, x, wq, wkv, wku, wvu, wo, wfc, wproj, c_idf, c_idh, c_idb, c_mask0, c_mask1,
                 c_msink, c_bias, c_mov, c_rowlo, c_gmask, c_vsmask, c_vsones, out):
    fp32, fp32r = mybir.dt.float32, mybir.dt.float32r
    bf16, fp16 = mybir.dt.bfloat16, mybir.dt.float16
    ALU = mybir.AluOpType
    ACT = mybir.ActivationFunctionType
    AX = mybir.AxisListType

    ctx = ExitStack()
    with ctx:
        def sb(name, shape, dt):
            return ctx.enter_context(nc.sbuf_tensor(name, shape, dt))

        def sem(name):
            return ctx.enter_context(nc.semaphore(name))

        idf = sb("idf", [P, P], fp32)
        idh = sb("idh", [P, P], fp16)
        idb = sb("idb", [P, P], bf16)
        mask0 = sb("mask0", [P, P], bf16)
        mask1 = sb("mask1", [P, T - BLK], bf16)
        msink = sb("msink", [P, H * SINK], bf16)
        bias = sb("bias", [BIAS_ROWS, 2 * H + 1, P], bf16)
        mov = sb("mov", [BIAS_ROWS, T], bf16)
        rowlo = sb("rowlo", [P, 1], fp32)
        gmask = sb("gmask", [P, G], fp32)
        vsmask = sb("vsmask", [H * SINK, H], fp32)
        ones = sb("ones", [P, P], fp32)
        neghalf = sb("neghalf", [P, 2], fp32)
        wq_r = sb("wq_r", [P, CC, C], fp32)
        wkv_r = sb("wkv_r", [L, C], fp32)
        wku_r = sb("wku_r", [P, CC, L], fp32)
        wvu_r = sb("wvu_r", [P, CC, L], fp32)
        wo_r = sb("wo_r", [P, CC, C], fp32)
        wfc_r = sb("wfc_r", [P, FC, C], fp32)
        wpr_r = sb("wpr_r", [P, CC, F], fp32)
        wqT = sb("wqT", [P, CC, H, 2, HD], fp32)
        wkvT = sb("wkvT", [P, CC, L], fp32)
        wkT = sb("wkT", [L, H, 2, HD], fp32)
        wvT = sb("wvT", [L, C], fp32)
        woT = sb("woT", [P, CC, C], fp32)
        neg_t = sb("neg_t", [P, FC * C], fp16)
        tern = sb("tern", [P, FC * C], fp16)
        fcT = sb("fcT", [P, CC, F], fp16)
        prT = sb("prT", [P, FC, C], fp16)
        wsum = sb("wsum", [P, 2, FC], fp32)
        gam = sb("gam", [P, 2], fp32)
        thr = sb("thr", [P, 2], fp32)
        nthr = sb("nthr", [P, 2], fp32)
        gam128 = sb("gam128", [P, 2], fp32)
        xin = sb("xin", [P, TT_, C], fp32)
        st1 = sb("st1", [P, TT_, 6], fp32)
        mv1 = sb("mv1", [P, TT_, 2], fp32)
        ve1 = sb("ve1", [P, TT_], fp32)
        rs1 = sb("rs1", [P, TT_], fp32)
        xn = sb("xn", [P, TT_, C], fp32)
        st2 = sb("st2", [P, TT_, 6], fp32)
        mv2 = sb("mv2", [P, TT_, 2], fp32)
        ve2 = sb("ve2", [P, TT_], fp32)
        rs2 = sb("rs2", [P, TT_], fp32)
        cx = sb("cx", [P, TT_, C], fp32)
        gx = sb("gx", [P, TT_], fp32)
        gxr = sb("gxr", [P, TT_], fp32)
        ga1 = sb("ga1", [P, TT_], fp32)
        a1 = sb("a1", [P, TT_], fp32)
        txs = sb("txs", [P, TT_, C], fp32)
        xnT = sb("xnT", [P, CC, T], fp32)
        thT = sb("thT", [P, CC, T], fp16)
        tlT = sb("tlT", [P, CC, T], fp16)
        latT = sb("latT", [L, T], fp32)
        latS = sb("latS", [L, H, SINK], fp32)
        qh = sb("qh", [P, NT * T], fp32r)
        Q = sb("Q", [P, NT, T], fp32r)
        KH = sb("KH", [P, NT, T], fp32r)
        KL = sb("KL", [P, NT, T], fp32r)
        BDH = sb("BDH", [P, NT, P], fp32r)
        BDL = sb("BDL", [P, NT, P], fp32r)
        V = sb("V", [P, 3, H, VW], fp32)
        VS = sb("VS", [H * SINK, H, VW], fp32)
        mx = sb("mx", [P, TT_, H], fp32)
        smx = sb("smx", [P, TT_, H], fp32)
        mm = sb("mm", [P, TT_, H], fp32)
        mhl = sb("mhl", [P, TT_, 2, H], bf16)
        E = sb("E", [P, G, NT, T], fp32)
        ES = sb("ES", [H * SINK, T], fp32)
        rden = sb("rden", [P, TT_, H], fp32)
        y = sb("y", [P, TT_, C], fp32)
        yT = sb("yT", [P, CC, T], fp32)
        xres = sb("xres", [P, TT_, C], fp32)
        xat = sb("xat", [P, TT_, C], fp32)
        ob = sb("ob", [P, TT_, C], fp32)
        gl = sb("gl", [P, TT_, F], fp32)
        sth = sb("sth", [P, TT_, 2, 6], fp32)
        mvh = sb("mvh", [P, TT_, 2], fp32)
        veh = sb("veh", [P, TT_], fp32)
        rsh = sb("rsh", [P, TT_], fp32)
        ch = sb("ch", [P, TT_, F], fp32)
        gh = sb("gh", [P, TT_], fp32)
        ghr = sb("ghr", [P, TT_], fp32)
        ga2 = sb("ga2", [P, TT_], fp32)
        a2 = sb("a2", [P, TT_], fp32)
        t2h = sb("t2h", [P, TT_, FC, P], fp16)
        t2l = sb("t2l", [P, TT_, FC, P], fp16)

        ring = [ctx.enter_context(nc.psum_tensor(f"ring{i}", [P, 2, 512], fp32)) for i in range(3)]
        aux = ctx.enter_context(nc.psum_tensor("aux", [P, 512], fp32))
        acc = ctx.enter_context(nc.psum_tensor("acc", [P, 512], fp32))

        def stage(name, per):
            return sem(name), per, 0

        primed = []

        def primed_stage(name, per):
            primed.append(sem(name))
            return primed[-1], per, 1

        ld_const = sem("ld_const"); ld_wa = sem("ld_wa"); ld_wf = sem("ld_wf"); ld_wp = sem("ld_wp")
        ld_x = stage("ld_x", 16); ld_res = stage("ld_res", 16); st_out = primed_stage("st_out", 16)
        memsets = sem("memsets")
        passed = sem("passed")
        w_tr = sem("w_tr"); w_ev = sem("w_ev"); w_abs = sem("w_abs"); w_tot = sem("w_tot"); w_tern = sem("w_tern")
        dve_pro = sem("dve_pro")
        pool_pro = sem("pool_pro")
        tr_x = stage("tr_x", 1); mm_lat = stage("mm_lat", 1); mm_q = stage("mm_q", 1)
        mm_k = stage("mm_k", 1); mm_v = stage("mm_v", 1); mm_vs = stage("mm_vs", 1)
        xnT_ok = stage("xnT_ok", 1); th_ok = stage("th_ok", 1); tl_ok = stage("tl_ok", 1)
        lat_ok = stage("lat_ok", 2); qh_ok = stage("qh_ok", 1); q_ok = stage("q_ok", 1)
        kh_ok = stage("kh_ok", 1); kl_ok = stage("kl_ok", 1); bd_ok = stage("bd_ok", 2)
        v_ok = stage("v_ok", 1); vs_ok = stage("vs_ok", 1)
        var1 = stage("var1", TT_); rstd1 = stage("rstd1", 1); xn_ok = stage("xn_ok", TT_)
        gx_ok = stage("gx_ok", TT_); tx_ok = stage("tx_ok", TT_); a1_ok = stage("a1_ok", 1)
        pool_f = stage("pool_f", 4)
        s1 = stage("s1", 6); s1s = stage("s1s", 1); red1 = primed_stage("red1", 6); red1s = stage("red1s", 1)
        m_ok = stage("m_ok", 2); mT = primed_stage("mT", 1); mT_ok = stage("mT_ok", 1)
        s2 = stage("s2", 4); s2s = primed_stage("s2s", 1); ex = primed_stage("ex", 4); exs = stage("exs", 1)
        pv = primed_stage("pv", TT_); y_ok = stage("y_ok", TT_); tr_y = primed_stage("tr_y", 1)
        yT_ok = stage("yT_ok", 1); mm_wo = primed_stage("mm_wo", 1)
        fc = stage("fc", TT_); gelu = primed_stage("gelu", TT_); t2 = primed_stage("t2", TT_); gh_ok = stage("gh_ok", TT_)
        tr_h = stage("tr_h", TT_); t2h_ok = stage("t2h_ok", TT_); t2l_ok = primed_stage("t2l_ok", TT_)
        pr = primed_stage("pr", TT_); a2_ok = primed_stage("a2_ok", TT_); pool_b = stage("pool_b", 6)
        xa_ok = primed_stage("xa_ok", TT_); o_ok = primed_stage("o_ok", TT_)
        DF, DB = 9, 13
        dve_f = stage("dve_f", DF); dve_b = stage("dve_b", DB)

        def wait(eng, st, b, k=None):
            s, per, start = st
            v = b * per + (per if k is None else k) + start
            if not isinstance(v, int) or v > start:
                eng.wait_ge(s, v)

        def wait_before(eng, st, b):
            wait(eng, st, b, 0)

        def wait_apart(eng, st, b, k=None):
            wait(eng, st, b, k)
            if not isinstance(b, int):
                eng.sem_inc(passed, 1)

        x_v = x.rearrange("b (i p) c -> b p i c", p=P)
        out_v = out.rearrange("b (i p) c -> b p i c", p=P)

        USES = (
            [("p1", r, [(red1, r + 1)]) for r in range(6)]
            + [("fc", i, [(gelu, i + 1)]) for i in range(TT_)]
            + [("p2", r, [(ex, r + 1)]) for r in range(4)]
            + [("f_tr", 0, [(xnT_ok, 1), (th_ok, 1), (tl_ok, 1)]), ("f_q", 0, [(q_ok, 1)]),
               ("f_k", 0, [(kl_ok, 1)]), ("f_v", 0, [(v_ok, 1)])]
            + [("t2T", i, [(t2l_ok, i + 1)]) for i in range(TT_)]
        )
        NU = len(USES)
        assert NU % 3 == 0
        AT = {(n, i): u for u, (n, i, _) in enumerate(USES)}

        def take(eng, name, i, b, back, front):
            u = AT[(name, i)]
            v, cur = u, True
            while True:
                v -= 3
                if v < 0:
                    v += NU
                    if not cur:
                        break
                    cur = False
                is_front = USES[v][0].startswith("f_")
                if cur and not (front if is_front else back):
                    continue
                if not cur and not is_front and not back:
                    continue
                if not cur and is_front and not back:
                    break
                for st, k in USES[v][2]:
                    if cur:
                        wait(eng, st, b + 1 if is_front else b, k)
                    elif is_front:
                        wait(eng, st, b, k)
                    else:
                        wait_before(eng, st, b)
                break
            return ring[u % 3]

        def schedule(eng, body):
            body(-1, False, True)
            with eng.Fori(0, B - 1) as b:
                body(b, True, True)
            body(B - 1, True, False)

        block = ctx.enter_context(nc.Block())

        @block.sync
        def _(sp):
            sp.dma_start(xin[:], x_v[0]).then_inc(ld_x[0], 16)
            for dst, src in ((idf, c_idf), (mask0, c_mask0), (mask1, c_mask1), (msink, c_msink), (idb, c_idb),
                             (idh, c_idh), (rowlo, c_rowlo), (gmask, c_gmask), (vsmask, c_vsmask), (mov, c_mov),
                             (bias, c_bias)):
                view = dst[:].bitcast(mybir.dt.uint16) if dst.dtype == bf16 else dst[:]
                sp.dma_start(view, src).then_inc(ld_const, 16)
            sp.dma_start(VS[:], c_vsones).then_inc(ld_const, 16)

            def body(b, back, front):
                if front and back:
                    wait(sp, xn_ok, b)
                    sp.dma_start(xin[:], x_v[b + 1]).then_inc(ld_x[0], 16)
                if back:
                    wait_before(sp, xa_ok, b)
                    sp.dma_start(xres[:], x_v[b]).then_inc(ld_res[0], 16)
                    wait(sp, o_ok, b)
                    sp.dma_start(out_v[b], ob[:]).then_inc(st_out[0], 16)

            schedule(sp, body)
            wait(sp, st_out, B - 1)

        @block.gpsimd
        def _(pool):
            nc.gpsimd.memset(neghalf[:], -0.5).then_inc(memsets, 1)
            nc.gpsimd.memset(V[:], 1.0).then_inc(memsets, 1)
            nc.gpsimd.memset(ones[:], 1.0).then_inc(memsets, 1)
            pool.wait_ge(memsets, 3)
            for s in primed:
                pool.sem_inc(s, 1)

            def body(b, back, front):
                if front:
                    f = b + 1
                    wait_apart(pool, var1, f)
                    nc.gpsimd.tensor_scalar(ve1[:], mv1[:, :, 1], LN_EPS, None, ALU.add).then_inc(pool_f[0], 1)
                    wait(pool, pool_f, f, 1)
                    nc.gpsimd.tensor_tensor(rs1[:], ve1[:], neghalf[:], ALU.pow).then_inc(rstd1[0], 1)
                    wait_apart(pool, gx_ok, f)
                    nc.gpsimd.tensor_scalar(ve2[:], mv2[:, :, 1], FFN_EPS, None, ALU.add).then_inc(pool_f[0], 1)
                    wait(pool, pool_f, f, 2)
                    nc.gpsimd.tensor_tensor(rs2[:], ve2[:], neghalf[:], ALU.pow).then_inc(pool_f[0], 1)
                    wait(pool, pool_f, f, 3)
                    nc.gpsimd.tensor_tensor(ga1[:], rs2[:], gx[:], ALU.mult).then_inc(pool_f[0], 1)
                    if back:
                        wait(pool, gelu, b)
                    else:
                        pool.wait_ge(dve_pro, 4)
                    wait_apart(pool, pool_f, f, 4)
                    nc.gpsimd.tensor_scalar(a1[:], ga1[:], gam128[:, 0:1], None, ALU.mult).then_inc(a1_ok[0], 1)
                if back:
                    for i in range(TT_):
                        wait_apart(pool, gh_ok, b, i + 1)
                        nc.gpsimd.tensor_scalar(veh[:, i:i + 1], mvh[:, i, 1:2], FFN_EPS, None, ALU.add).then_inc(pool_b[0], 1)
                        wait(pool, pool_b, b, 3 * i + 1)
                        nc.gpsimd.tensor_tensor(rsh[:, i:i + 1], veh[:, i:i + 1], neghalf[:, 0:1], ALU.pow).then_inc(pool_b[0], 1)
                        wait(pool, pool_b, b, 3 * i + 2)
                        nc.gpsimd.tensor_tensor(ga2[:, i:i + 1], rsh[:, i:i + 1], gh[:, i:i + 1], ALU.mult).then_inc(pool_b[0], 1)
                        if i == 0:
                            wait_before(pool, o_ok, b)
                        wait_apart(pool, pool_b, b, 3 * i + 3)
                        nc.gpsimd.tensor_scalar(a2[:, i:i + 1], ga2[:, i:i + 1], gam128[:, 1:2], None, ALU.mult).then_inc(a2_ok[0], 1)

            schedule(pool, body)

        @block.scalar
        def _(act):
            for dst, src in ((wkv_r[:], wkv), (wq_r[:], wq.rearrange("(c p) k -> p c k", p=P)),
                             (wku_r[:], wku.rearrange("(c p) k -> p c k", p=P)),
                             (wvu_r[:], wvu.rearrange("(c p) k -> p c k", p=P)),
                             (wo_r[:], wo.rearrange("(c p) k -> p c k", p=P))):
                act.dma_start(dst, src).then_inc(ld_wa, 16)
            act.dma_start(wfc_r[:], wfc.rearrange("(c p) k -> p c k", p=P)).then_inc(ld_wf, 16)
            act.dma_start(wpr_r[:], wproj.rearrange("(c p) k -> p c k", p=P)).then_inc(ld_wp, 16)

            act.wait_ge(w_tr, 1)
            for c in range(CC):
                for d in range(2):
                    nc.scalar.activation(wqT[:, c, :, d, :], ring[0][:, c, 0:C].rearrange("p (h e) -> p h e", h=H),
                                         ACT.Copy, scale=float(HD) ** -0.5).then_inc(w_ev, 1)
            act.wait_ge(w_tr, 2)
            nc.scalar.activation(wkvT[:], ring[1][:, 0, 0:CC * L].rearrange("p (c l) -> p c l", c=CC), ACT.Copy).then_inc(w_ev, 1)
            for d in range(2):
                nc.scalar.activation(wkT[:, :, d, :], ring[1][0:L, 1, 0:C].rearrange("p (h e) -> p h e", h=H),
                                     ACT.Copy).then_inc(w_ev, 1)
            nc.scalar.activation(wvT[:], ring[1][0:L, 1, C:2 * C], ACT.Copy).then_inc(w_ev, 1)
            act.wait_ge(w_tr, 3)
            nc.scalar.activation(woT[:], ring[2][:, :, 0:C], ACT.Copy).then_inc(w_ev, 1)
            def body(b, back, front):
                f = b + 1
                if back:
                    for i in range(TT_):
                        wait(act, fc, b, i + 1)
                        if i == 0:
                            wait(act, a1_ok, b)
                            wait_before(act, t2, b)
                        nc.scalar.activation(gl[:, i, :], ring[AT[("fc", i)] % 3][:].rearrange("p a n -> p (a n)"),
                                             ACT.Gelu, scale=a1[:, i:i + 1]).then_inc(gelu[0], 1)
                    for r in range(4):
                        gp, tp = divmod(r, 2)
                        wait(act, s2, b, r + 1)
                        if r == 0:
                            wait_before(act, pv, b)
                        nc.scalar.activation(E[:, 2 * gp:2 * gp + 2, 2 * tp:2 * tp + 2, :].rearrange("p g t q -> p g (t q)"),
                                             ring[AT[("p2", r)] % 3][:], ACT.Exp).then_inc(ex[0], 1)
                    wait(act, s2s, b)
                    nc.scalar.activation(ES[:], aux[0:H * SINK, 0:T], ACT.Exp).then_inc(exs[0], 1)
                if front:
                    wait(act, tr_x, f)
                    src = ring[AT[("f_tr", 0)] % 3]
                    if back:
                        wait(act, mm_q, b)
                    nc.scalar.activation(xnT[:], src[:, 0, :].rearrange("p (c t) -> p c t", c=CC), ACT.Copy).then_inc(xnT_ok[0], 1)
                    if back:
                        wait(act, fc, b)
                    nc.scalar.activation(thT[:], src[:, 1, :].rearrange("p (c t) -> p c t", c=CC), ACT.Copy).then_inc(th_ok[0], 1)
                    wait(act, mm_lat, f)
                    if back:
                        wait(act, mm_vs, b)
                    nc.scalar.activation(latT[:], aux[0:L, 0:T], ACT.Copy).then_inc(lat_ok[0], 1)
                    nc.scalar.activation(latS[:], aux[0:L, 0:SINK].unsqueeze(1).to_broadcast([L, H, SINK]),
                                         ACT.Copy).then_inc(lat_ok[0], 1)
                    wait(act, mm_q, f)
                    if back:
                        wait(act, q_ok, b)
                    nc.scalar.activation(qh[:], ring[AT[("f_q", 0)] % 3][:].rearrange("p a n -> p (a n)"), ACT.Copy).then_inc(qh_ok[0], 1)
                    wait(act, mm_k, f)
                    if back:
                        wait(act, s2s, b)
                    nc.scalar.activation(KH[:].rearrange("p t n -> p (t n)"), ring[AT[("f_k", 0)] % 3][:].rearrange("p a n -> p (a n)"),
                                         ACT.Copy).then_inc(kh_ok[0], 1)
                    wait(act, mm_v, f)
                    if back:
                        wait(act, pv, b)
                    else:
                        act.wait_ge(memsets, 3)
                    slot = ring[AT[("f_v", 0)] % 3]
                    nc.scalar.activation(V[:, :, :, 0:HD], slot[:].rearrange("p a n -> p (a n)")[:, 0:3 * C]
                                         .rearrange("p (j h d) -> p j h d", j=3, h=H), ACT.Copy).then_inc(v_ok[0], 1)
                if back:
                    for i in range(TT_):
                        wait(act, tr_h, b, i + 1)
                        if i == 0:
                            wait_before(act, pr, b)
                        nc.scalar.activation(t2h[:, i].rearrange("p k n -> p (k n)"), ring[AT[("t2T", i)] % 3][:].rearrange("p a n -> p (a n)"),
                                             ACT.Copy).then_inc(t2h_ok[0], 1)
                    wait(act, tr_y, b)
                    wait_before(act, mm_wo, b)
                    nc.scalar.activation(yT[:], aux[:].rearrange("p (c t) -> p c t", c=CC), ACT.Copy).then_inc(yT_ok[0], 1)

            def weights():
                act.wait_ge(ld_wf, 16)
                for c in range(FC):
                    nc.scalar.activation(tern[:, c * C:(c + 1) * C], wfc_r[:, c, :], ACT.Abs, accum_out=wsum[:, 0, c:c + 1]).then_inc(w_abs, 1)
                act.wait_ge(ld_wp, 16)
                for c in range(FC):
                    nc.scalar.activation(neg_t[:, c * C:(c + 1) * C], wpr_r[:, c // 4, (c % 4) * C:(c % 4 + 1) * C], ACT.Abs,
                                         accum_out=wsum[:, 1, c:c + 1]).then_inc(w_abs, 1)
                for c in range(CC):
                    act.wait_ge(w_tr, 4 + c)
                    nc.scalar.activation(fcT[:, c, :], ring[c][:, 0, :].bitcast(fp16), ACT.Copy).then_inc(w_ev, 1)
                for j in range(2):
                    act.wait_ge(w_tr, 6 + j)
                    nc.scalar.activation(prT[:, 4 * j:4 * j + 4, :], ring[(2 + j) % 3][:, 0, :].bitcast(fp16)
                                         .rearrange("p (k c) -> p k c", k=4), ACT.Copy).then_inc(w_ev, 1)

            first = [True]

            def with_weights(b, back, front):
                body(b, back, front)
                if first[0]:
                    first[0] = False
                    weights()

            schedule(act, with_weights)

        @block.vector
        def _(dve):
            def flat(t):
                return t.rearrange("p a n -> p (a n)")

            nc.vector.memset(BDH[:].bitcast(fp32), 0.0).then_inc(dve_pro, 1)
            nc.vector.memset(BDL[:].bitcast(fp32), 0.0).then_inc(dve_pro, 1)

            def weights():
                dve.wait_ge(w_tot, 1)
                nc.vector.tensor_reduce(out=gam[:], in_=acc[:, 0:2 * FC].rearrange("p (a c) -> p a c", a=2), axis=AX.X, op=ALU.add).then_inc(dve_pro, 1)
                dve.wait_ge(dve_pro, 3)
                nc.vector.tensor_scalar(gam128[:], gam[:], 1.0 / (F * C * QB), None, ALU.mult).then_inc(dve_pro, 1)
                nc.vector.tensor_scalar(thr[:], gam[:], 1.0 / (F * C), FFN_EPS, ALU.mult, ALU.add).then_inc(dve_pro, 1)
                dve.wait_ge(dve_pro, 5)
                nc.vector.tensor_scalar(nthr[:], thr[:], -0.5, None, ALU.mult).then_inc(dve_pro, 1)
                nc.vector.tensor_scalar(thr[:], thr[:], 0.5, None, ALU.mult).then_inc(dve_pro, 1)
                dve.wait_ge(dve_pro, 7)
                for n, w in enumerate((flat(wfc_r), flat(wpr_r))):
                    if n:
                        dve.wait_ge(w_tr, 5)
                    nc.vector.tensor_scalar(neg_t[:], w, nthr[:, n:n + 1], None, ALU.is_lt).then_inc(dve_pro, 1)
                    dve.wait_ge(dve_pro, 8 + n)
                    nc.vector.scalar_tensor_tensor(out=tern[:], in0=w, scalar=thr[:, n:n + 1], in1=neg_t[:],
                                                   op0=ALU.is_gt, op1=ALU.subtract).then_inc(w_tern, 1)

            def body(b, back, front):
                f = b + 1
                steps = {"f": 0, "b": 0}

                def did(ins, w):
                    steps[w] += 1
                    ins.then_inc((dve_f if w == "f" else dve_b)[0], 1)

                def settle(w, how=wait):
                    how(dve, dve_f if w == "f" else dve_b, f if w == "f" else b, steps[w])

                if back:
                    for r in range(6):
                        wait(dve, s1, b, r + 1)
                        src = ring[AT[("p1", r)] % 3]
                        if r < 2:
                            nc.vector.tensor_reduce(out=mx[:, 0, 8 * r:8 * r + 8], in_=src[:].rearrange("p a (t k) -> p (a t) k", t=NT),
                                                    axis=AX.X, op=ALU.max).then_inc(red1[0], 1)
                        else:
                            gp, tp = divmod(r - 2, 2)
                            o = mx[:, 1, :].rearrange("p (g t) -> p g t", g=G)[:, 2 * gp:2 * gp + 2, 2 * tp:2 * tp + 2]
                            nc.vector.tensor_reduce(out=o, in_=src[:, :, 0:2 * (T - BLK)].rearrange("p a (t k) -> p a t k", t=2),
                                                    axis=AX.X, op=ALU.max).then_inc(red1[0], 1)
                    wait(dve, s1s, b)
                    nc.vector.tensor_reduce(out=flat(smx), in_=aux[:, 0:TT_ * H * SINK].rearrange("p (h s) -> p h s", s=SINK),
                                            axis=AX.X, op=ALU.max).then_inc(red1s[0], 1)
                    wait(dve, red1, b)
                    wait(dve, red1s, b)
                    did(nc.vector.tensor_tensor(flat(mm), flat(mx), flat(smx), ALU.max), "b")
                    settle("b")
                    wait_before(dve, mT, b)
                    nc.vector.tensor_scalar(mhl[:, :, 0, :], mm[:], -1.0, None, ALU.mult).then_inc(m_ok[0], 1)
                    wait(dve, m_ok, b, 1)
                    nc.vector.scalar_tensor_tensor(out=mhl[:, :, 1, :], in0=mm[:], scalar=-1.0, in1=mhl[:, :, 0, :],
                                                   op0=ALU.mult, op1=ALU.subtract).then_inc(m_ok[0], 1)
                    wait(dve, mT, b)
                    wait_before(dve, s2s, b)
                    nc.vector.tensor_copy(mov[BLK:BLK + 2 * H, :], aux[BLK:BLK + 2 * H, 0:T // 2].bitcast(bf16)).then_inc(mT_ok[0], 1)
                if front:
                    wait(dve, ld_x, f)
                    for i in range(TT_):
                        did(nc.vector.bn_stats(st1[:, i, :], xin[:, i, :]), "f")
                    settle("f", wait_apart)
                    for i in range(TT_):
                        nc.vector.bn_aggr(mv1[:, i, :], st1[:, i, :]).then_inc(var1[0], 1)
                    wait(dve, rstd1, f)
                    wait(dve, var1, f)
                    if back:
                        wait(dve, tr_x, b)
                    for i in range(TT_):
                        nc.vector.tensor_scalar(xn[:, i, :], xin[:, i, :], mv1[:, i, 0:1], rs1[:, i:i + 1],
                                                ALU.subtract, ALU.mult).then_inc(xn_ok[0], 1)
                    wait(dve, xn_ok, f)
                    for i in range(TT_):
                        did(nc.vector.bn_stats(st2[:, i, :], xn[:, i, :]), "f")
                    settle("f", wait_apart)
                    for i in range(TT_):
                        did(nc.vector.bn_aggr(mv2[:, i, :], st2[:, i, :]), "f")
                    settle("f")
                    for i in range(TT_):
                        did(nc.vector.tensor_scalar(cx[:, i, :], xn[:, i, :], mv2[:, i, 0:1], None, ALU.subtract), "f")
                    settle("f")
                    if back:
                        wait(dve, a1_ok, b)
                    for i in range(TT_):
                        nc.vector.tensor_reduce(out=gx[:, i:i + 1], in_=cx[:, i, :], axis=AX.X, op=ALU.max,
                                                apply_absolute_value=True).then_inc(gx_ok[0], 1)
                    wait(dve, gx_ok, f)
                    did(nc.vector.reciprocal(gxr[:], gx[:]), "f")
                    settle("f")
                    for i in range(TT_):
                        nc.vector.tensor_scalar(txs[:, i, :], cx[:, i, :], gxr[:, i:i + 1], QB, ALU.mult, ALU.mult).then_inc(tx_ok[0], 1)
                if back:
                    for i in range(TT_):
                        wait(dve, gelu, b, i + 1)
                        for j in range(2):
                            did(nc.vector.bn_stats(sth[:, i, j, :], gl[:, i, 512 * j:512 * j + 512]), "b")
                        settle("b", wait_apart)
                        did(nc.vector.bn_aggr(mvh[:, i, :], flat(sth[:, i])), "b")
                        settle("b")
                        did(nc.vector.tensor_scalar(ch[:, i, :], gl[:, i, :], mvh[:, i, 0:1], None, ALU.subtract), "b")
                        settle("b")
                        if i == 0:
                            wait_before(dve, a2_ok, b)
                        nc.vector.tensor_reduce(out=gh[:, i:i + 1], in_=ch[:, i, :], axis=AX.X, op=ALU.max,
                                                apply_absolute_value=True).then_inc(gh_ok[0], 1)
                        wait(dve, gh_ok, b, i + 1)
                        did(nc.vector.reciprocal(ghr[:, i:i + 1], gh[:, i:i + 1]), "b")
                        settle("b")
                        nc.vector.tensor_scalar(ch[:, i, :], ch[:, i, :], ghr[:, i:i + 1], QB, ALU.mult, ALU.mult).then_inc(t2[0], 1)
                if back:
                    for i in range(TT_):
                        wait(dve, pv, b, i + 1)
                        o = (acc if i == 0 else aux)[:, 0:H * VW].rearrange("p (h d) -> p h d", h=H)
                        did(nc.vector.reciprocal(rden[:, i, :], o[:, :, HD]), "b")
                        settle("b")
                        if i == 0:
                            wait_before(dve, tr_y, b)
                        nc.vector.tensor_tensor(y[:, i, :].rearrange("p (h d) -> p h d", h=H), o[:, :, 0:HD],
                                                rden[:, i, :].unsqueeze(2).to_broadcast([P, H, HD]), ALU.mult).then_inc(y_ok[0], 1)
                if front:
                    wait(dve, tr_x, f)
                    src = ring[AT[("f_tr", 0)] % 3]
                    wait(dve, th_ok, f)
                    nc.vector.tensor_tensor(tlT[:], src[:, 1, :].rearrange("p (c t) -> p c t", c=CC), thT[:], ALU.subtract).then_inc(tl_ok[0], 1)
                    wait(dve, qh_ok, f)
                    if not back:
                        dve.wait_ge(ld_const, 16 * 12)
                    nc.vector.scalar_tensor_tensor(out=flat(Q), in0=qh[:].bitcast(fp32), scalar=rowlo[:, 0:1],
                                                   in1=ring[AT[("f_q", 0)] % 3][:].rearrange("p a n -> p (a n)"),
                                                   op0=ALU.mult, op1=ALU.add).then_inc(q_ok[0], 1)
                    wait(dve, kh_ok, f)
                    nc.vector.tensor_tensor(flat(KL), ring[AT[("f_k", 0)] % 3][:].rearrange("p a n -> p (a n)"),
                                            flat(KH).bitcast(fp32), ALU.subtract).then_inc(kl_ok[0], 1)
                    wait(dve, kl_ok, f)
                    for d, s in ((BDH, KH), (BDL, KL)):
                        o = flat(d).rearrange("p (t n) -> p t n", t=NT)
                        o = bass.AP(o.tensor, o.offset, [o.ap[0], [P + SINK, NT], [NT * SINK, G], [1, SINK]])
                        nc.vector.tensor_tensor(o, s[:, :, 0:SINK].bitcast(fp32).unsqueeze(2).to_broadcast([P, NT, G, SINK]),
                                                gmask[:].unsqueeze(1).unsqueeze(3).to_broadcast([P, NT, G, SINK]), ALU.mult).then_inc(bd_ok[0], 1)
                    wait(dve, mm_vs, f)
                    nc.vector.tensor_tensor(VS[:, :, 0:HD], aux[0:H * SINK, 0:C].rearrange("p (h d) -> p h d", h=H),
                                            vsmask[:].unsqueeze(2).to_broadcast([H * SINK, H, HD]), ALU.mult).then_inc(vs_ok[0], 1)
                if back:
                    for i in range(TT_):
                        wait(dve, t2h_ok, b, i + 1)
                        nc.vector.tensor_tensor(t2l[:, i].rearrange("p k n -> p (k n)"), ring[AT[("t2T", i)] % 3][:].rearrange("p a n -> p (a n)"),
                                                t2h[:, i].rearrange("p k n -> p (k n)"), ALU.subtract).then_inc(t2l_ok[0], 1)
                    wait(dve, mm_wo, b)
                    wait(dve, ld_res, b)
                    for i in range(TT_):
                        nc.vector.tensor_tensor(xat[:, i, :], aux[:, i * C:(i + 1) * C], xres[:, i, :], ALU.add).then_inc(xa_ok[0], 1)
                    wait(dve, xa_ok, b)
                    wait_before(dve, st_out, b)
                    for i in range(TT_):
                        wait(dve, pr, b, i + 1)
                        wait(dve, a2_ok, b, i + 1)
                        nc.vector.scalar_tensor_tensor(out=ob[:, i, :], in0=acc[:, i * C:(i + 1) * C], scalar=a2[:, i:i + 1],
                                                       in1=xat[:, i, :], op0=ALU.mult, op1=ALU.add).then_inc(o_ok[0], 1)
                assert not front or steps["f"] == DF, steps
                assert not back or steps["b"] == DB, steps

            first = [True]

            def with_weights(b, back, front):
                body(b, back, front)
                if first[0]:
                    first[0] = False
                    weights()

            schedule(dve, with_weights)

        @block.tensor
        def _(pe):
            pe.wait_ge(ld_const, 16 * 12)
            pe.wait_ge(ld_wa, 16 * 5)
            for c in range(CC):
                for r in range(CC):
                    last = nc.tensor.transpose(ring[0][:, c, r * P:(r + 1) * P], wq_r[:, r, c * P:(c + 1) * P], idf[:])
            last.then_inc(w_tr, 1)
            for c in range(CC):
                nc.tensor.transpose(ring[1][:, 0, c * L:(c + 1) * L], wkv_r[:, c * P:(c + 1) * P], idf[0:L, 0:L])
            for n, w in enumerate((wku_r, wvu_r)):
                for r in range(CC):
                    last = nc.tensor.transpose(ring[1][0:L, 1, n * C + r * P:n * C + (r + 1) * P], w[:, r, :], idf[:])
            last.then_inc(w_tr, 1)
            for c in range(CC):
                for r in range(CC):
                    last = nc.tensor.transpose(ring[2][:, c, r * P:(r + 1) * P], wo_r[:, r, c * P:(c + 1) * P], idf[:])
            last.then_inc(w_tr, 1)
            N_EV = 4 + 1 + 2 + 1 + 1

            def weights():
                pe.wait_ge(w_abs, 2 * FC)
                pe.wait_ge(memsets, 3)
                nc.tensor.matmul(acc[:, 0:2 * FC], ones[:], flat(wsum), start=True, stop=True).then_inc(w_tot, 1)
                wait(pe, v_ok, 0)
                wait(pe, kl_ok, 0)
                wait(pe, q_ok, 0)
                pe.wait_ge(w_tern, 1)
                for c in range(CC):
                    for k in range(FC):
                        last = nc.tensor.transpose(ring[c][:, 0, :].bitcast(fp16)[:, k * P:(k + 1) * P],
                                                   tern[:, k * C + c * P:k * C + (c + 1) * P], idh[:])
                    last.then_inc(w_tr, 1)
                pe.wait_ge(w_tern, 2)
                for j in range(2):
                    pe.wait_ge(w_ev, N_EV + j)
                    for k in range(4):
                        for c in range(CC):
                            last = nc.tensor.transpose(ring[(2 + j) % 3][:, 0, :].bitcast(fp16)[:, k * C + c * P:k * C + (c + 1) * P],
                                                       tern[:, c * F + (4 * j + k) * P:c * F + (4 * j + k + 1) * P], idh[:])
                    last.then_inc(w_tr, 1)
                pe.wait_ge(w_ev, N_EV + 4)

            def flat(t):
                return t.rearrange("p a n -> p (a n)")

            def body(b, back, front):
                f = b + 1

                def slot(name, i=0):
                    return take(pe, name, i, b, back, front)

                def fc_tile(i):
                    if i == 0:
                        wait(pe, th_ok, b); wait(pe, tl_ok, b)
                    s = slot("fc", i)
                    for n in range(2):
                        for m, (c, src) in enumerate([(c, src) for src in (thT, tlT) for c in range(CC)]):
                            last = nc.tensor.matmul(s[:, n, :], src[:, c, i * P:(i + 1) * P], fcT[:, c, 512 * n:512 * n + 512],
                                                    start=(m == 0), stop=(m == 2 * CC - 1))
                    last.then_inc(fc[0], 1)

                if back:
                    wait(pe, q_ok, b); wait(pe, kh_ok, b)
                    for r in range(6):
                        s = slot("p1", r)
                        q0, k0, heads, mask = (0, 0, range(NT), mask0) if r < 2 else (P, BLK, range(2 * (r % 2), 2 * (r % 2) + 2), mask1)
                        n, gp = mask.shape[1], (r if r < 2 else (r - 2) // 2)
                        for a in range(2):
                            nc.tensor.matmul(s[:, a, 0:n * len(heads)].rearrange("p (t k) -> p t k", t=len(heads)), idb[:],
                                             mask[:].unsqueeze(1).to_broadcast([P, len(heads), n]), start=True, stop=False, skip_group_check=True)
                        for j, t in enumerate(heads):
                            for a in range(2):
                                g = 32 * (2 * gp + a)
                                last = nc.tensor.matmul(s[:, a, n * j:n * j + n], Q[g:g + 32, t, q0:q0 + P], KH[g:g + 32, t, k0:k0 + n],
                                                        start=False, stop=True, skip_group_check=True)
                        last.then_inc(s1[0], 1)
                    wait(pe, bd_ok, b)
                    wait(pe, vs_ok, b)
                    nc.tensor.matmul(aux[:, 0:H * SINK], idb[:], msink[:], start=True, stop=False, skip_group_check=True)
                    for i in range(TT_):
                        for t in range(NT):
                            last = nc.tensor.matmul(aux[:, i * H * SINK:(i + 1) * H * SINK], Q[:, t, i * P:(i + 1) * P], BDH[:, t, 0:H * SINK],
                                                    start=False, stop=(t == NT - 1), skip_group_check=True)
                    last.then_inc(s1s[0], 1)
                    fc_tile(0)
                    wait(pe, m_ok, b)
                    for i in range(TT_):
                        last = nc.tensor.transpose(aux[BLK:BLK + 2 * H, 0:T // 2].bitcast(bf16)[:, i * P:(i + 1) * P],
                                                   mhl[:, i].rearrange("p a h -> p (a h)"), idb[:])
                    last.then_inc(mT[0], 1)
                    fc_tile(1)
                    wait(pe, mT_ok, b); wait(pe, kl_ok, b)
                    for r in range(4):
                        gp, tp = divmod(r, 2)
                        s = slot("p2", r)
                        for j in range(2):
                            for a in range(2):
                                hm = NT * (2 * gp + a) + 2 * tp + j
                                nc.tensor.matmul(s[:, a, T * j:T * j + BLK], bias[:, hm, :], mov[:, 0:BLK],
                                                 start=(j == 0), stop=False, skip_group_check=True)
                                nc.tensor.matmul(s[:, a, T * j + BLK:T * j + T], bias[:, H + hm, :], mov[:, BLK:T],
                                                 start=False, stop=False, skip_group_check=True)
                        for j in range(2):
                            t = 2 * tp + j
                            for q0, n, k0 in ((0, P, 0), (P, BLK, BLK), (P + BLK, BLK, P)):
                                for K in (KH, KL):
                                    for a in range(2):
                                        g = 32 * (2 * gp + a)
                                        last = nc.tensor.matmul(s[:, a, T * j + q0:T * j + q0 + n], K[g:g + 32, t, k0:k0 + P],
                                                                Q[g:g + 32, t, q0:q0 + n], start=False, stop=True, skip_group_check=True)
                        last.then_inc(s2[0], 1)
                    nc.tensor.matmul(aux[:, 0:T], bias[:, 2 * H, :], mov[:], start=True, stop=False, skip_group_check=True)
                    for t in range(NT):
                        for K in (BDH, BDL):
                            last = nc.tensor.matmul(aux[:, 0:T], K[:, t, :], Q[:, t, :], start=False,
                                                    stop=(t == NT - 1 and K is BDL), skip_group_check=True)
                    last.then_inc(s2s[0], 1)
                if front:
                    s = slot("f_tr")
                    if not back:
                        pe.wait_ge(w_ev, N_EV)
                    wait(pe, xn_ok, f)
                    for c in range(CC):
                        for i in range(TT_):
                            nc.tensor.transpose(s[:, 0, c * T + i * P:c * T + (i + 1) * P], xn[:, i, c * P:(c + 1) * P], idf[:])
                    wait(pe, tx_ok, f)
                    for c in range(CC):
                        for i in range(TT_):
                            last = nc.tensor.transpose(s[:, 1, c * T + i * P:c * T + (i + 1) * P], txs[:, i, c * P:(c + 1) * P], idf[:])
                    last.then_inc(tr_x[0], 1)
                if back:
                    wait(pe, exs, b)
                    wait(pe, ex, b)
                    wait_before(pe, o_ok, b)
                    for i, o in ((0, acc), (1, aux)):
                        nc.tensor.matmul(o[:, 0:H * VW], ES[:, i * P:(i + 1) * P], VS[:].rearrange("p h d -> p (h d)"),
                                         start=True, stop=False, skip_group_check=True)
                        for h in range(H):
                            t, g = divmod(h, G)
                            parts = ((0, P, 0, 0),) if i == 0 else ((0, BLK, P, 1), (BLK, BLK, P + BLK, 2))
                            for p0, m, q0, v in parts:
                                last = nc.tensor.matmul(o[p0:p0 + m, h * VW:(h + 1) * VW], E[:, g, t, q0:q0 + m], V[:, v, h, :],
                                                        start=False, stop=True, skip_group_check=True)
                        last.then_inc(pv[0], 1)
                if front:
                    wait(pe, xnT_ok, f)
                    if back:
                        wait(pe, y_ok, b)
                    for c in range(CC):
                        last = nc.tensor.matmul(aux[0:L, 0:T], wkvT[:, c, :], xnT[:, c, :], start=(c == 0), stop=(c == CC - 1))
                    last.then_inc(mm_lat[0], 1)
                    s = slot("f_q")
                    for t in range(NT):
                        for c in range(CC):
                            last = nc.tensor.matmul(s[:, t // 2, (t % 2) * T:(t % 2 + 1) * T],
                                                    wqT[:, c, G * t:G * t + G].rearrange("p h d e -> p (h d e)"), xnT[:, c, :],
                                                    start=(c == 0), stop=(c == CC - 1), skip_group_check=True)
                    last.then_inc(mm_q[0], 1)
                    wait(pe, lat_ok, f)
                    s = slot("f_k")
                    for t in range(NT):
                        last = nc.tensor.matmul(s[:, t // 2, (t % 2) * T:(t % 2 + 1) * T],
                                                wkT[:, G * t:G * t + G].rearrange("p h d e -> p (h d e)"), latT[:], start=True, stop=True)
                    last.then_inc(mm_k[0], 1)
                    s = slot("f_v")
                    for j in range(3):
                        last = nc.tensor.matmul(s[:, j // 2, (j % 2) * C:(j % 2 + 1) * C], latT[:, BLK * j:BLK * j + P],
                                                wvT[:], start=True, stop=True)
                    last.then_inc(mm_v[0], 1)
                    nc.tensor.matmul(aux[0:H * SINK, 0:C], latS[:].rearrange("p h s -> p (h s)"), wvT[:],
                                     start=True, stop=True).then_inc(mm_vs[0], 1)
                if back:
                    for i in range(TT_):
                        wait(pe, t2, b, i + 1)
                        s = slot("t2T", i)
                        for k in range(FC):
                            last = nc.tensor.transpose(s[:, k // 4, (k % 4) * P:(k % 4 + 1) * P], ch[:, i, k * P:(k + 1) * P], idf[:])
                        last.then_inc(tr_h[0], 1)
                    wait(pe, y_ok, b)
                    if front:
                        wait(pe, vs_ok, f)
                    for c in range(CC):
                        for i in range(TT_):
                            last = nc.tensor.transpose(aux[:, c * T + i * P:c * T + (i + 1) * P], y[:, i, c * P:(c + 1) * P], idf[:])
                    last.then_inc(tr_y[0], 1)
                    for i in range(TT_):
                        wait(pe, t2h_ok, b, i + 1)
                        wait(pe, t2l_ok, b, i + 1)
                        for k in range(FC):
                            for src in (t2h, t2l):
                                last = nc.tensor.matmul(acc[:, i * C:(i + 1) * C], src[:, i, k, :], prT[:, k, :],
                                                        start=(k == 0 and src is t2h), stop=(k == FC - 1 and src is t2l), skip_group_check=True)
                        last.then_inc(pr[0], 1)
                    wait(pe, yT_ok, b)
                    for i in range(TT_):
                        for c in range(CC):
                            last = nc.tensor.matmul(aux[:, i * C:(i + 1) * C], yT[:, c, i * P:(i + 1) * P], woT[:, c, :],
                                                    start=(c == 0), stop=(c == CC - 1), skip_group_check=True)
                    last.then_inc(mm_wo[0], 1)

            first = [True]

            def with_weights(b, back, front):
                body(b, back, front)
                if first[0]:
                    first[0] = False
                    weights()

            schedule(pe, with_weights)


def shape_constants():
    import numpy as np

    def bf16_bits(a):
        return (np.ascontiguousarray(a, np.float32).view(np.uint32) >> 16).astype(np.uint16)

    k = {}
    k["c_idf"] = np.eye(P, dtype=np.float32)
    k["c_idh"] = np.eye(P, dtype=np.float16)
    k["c_idb"] = bf16_bits(np.eye(P))
    q, j = np.arange(T)[:, None], np.arange(T)[None, :]
    band = (j <= q) & (j >= q - (WINDOW - 1))
    mask = np.where(band, 0.0, MASKED)
    k["c_mask0"] = bf16_bits(mask[0:P, 0:P])
    k["c_mask1"] = bf16_bits(mask[P:T, BLK:T])
    sink = np.where(np.arange(SINK)[None, :] <= q - WINDOW, 0.0, MASKED)
    k["c_msink"] = bf16_bits(np.tile(sink[0:P], (1, H)))
    bias = np.zeros((BIAS_ROWS, 2 * H + 1, P), np.float32)
    for hm in range(H):
        bias[0:BLK, hm] = mask[0:BLK, 0:P]
        bias[0:BLK, H + hm] = mask[BLK:P, 0:P]
        for n in (hm, H + hm):
            bias[BLK + hm, n] = bias[BLK + H + hm, n] = 1.0
        bias[BLK + hm, 2 * H, hm * SINK:(hm + 1) * SINK] = 1.0
        bias[BLK + H + hm, 2 * H, hm * SINK:(hm + 1) * SINK] = 1.0
        for s in range(SINK):
            bias[BLK + 2 * H + s, 2 * H, hm * SINK + s] = MASKED
    k["c_bias"] = bf16_bits(bias)
    mov = np.zeros((BIAS_ROWS, T), np.float32)
    mov[0:BLK] = np.tile(np.eye(BLK), (1, T // BLK))
    mov[BLK + 2 * H:] = (sink != 0).T
    k["c_mov"] = bf16_bits(mov)
    p = np.arange(P)
    k["c_rowlo"] = -((p % 32) >= HD).astype(np.float32)[:, None]
    k["c_gmask"] = (p[:, None] // 32 == np.arange(G)[None, :]).astype(np.float32)
    hm = np.arange(H * SINK) // SINK
    own = ((hm % NT) * G + hm // NT)[:, None] == np.arange(H)[None, :]
    k["c_vsmask"] = own.astype(np.float32)
    k["c_vsones"] = np.zeros((H * SINK, H, VW), np.float32)
    k["c_vsones"][:, :, HD] = own
    return k


_INS = ["L0_attn_x", "L0_attn_Wq", "L0_attn_Wkv_down", "L0_attn_Wk_up", "L0_attn_Wv_up", "L0_attn_Wo",
        "L0_ffn_w_fc", "L0_ffn_w_proj"]


def kernel(**inputs):
    import numpy as np
    import concourse.bacc as bacc
    from concourse.bass_utils import run_bass_kernel_spmd

    nc = bacc.Bacc("TRN2", target_bir_lowering=False, num_devices=1)
    arrays, args = {}, []
    given = {name: np.ascontiguousarray(inputs[name]) for name in _INS}
    for name, a in {**given, **shape_constants()}.items():
        arrays[f"in_{name}"] = a
        args.append(nc.dram_tensor(f"in_{name}", a.shape, mybir.dt.from_np(a.dtype), kind="ExternalInput").ap())
    args.append(nc.dram_tensor("out_0", (B, T, C), mybir.dt.float32, kind="ExternalOutput").ap())
    layer_kernel(nc, *args)
    r = run_bass_kernel_spmd(nc, [arrays], core_ids=[0])
    return r.results[0]["out_0"]
```

```python
import concourse.bass as bass
from concourse import mybir
from contextlib import ExitStack

B, T, C, L, H, F = 4, 256, 256, 64, 16, 1024
HD = C // H
P = 128
WINDOW, SINK = 64, 4
TT_ = T // P
CC = C // P
FC = F // P
G = 4
NT = H // G
BLK = 64
VW = HD + 1
QB = 128.0
LN_EPS, FFN_EPS = 1e-5, 1e-6
BIAS_ROWS = BLK + 2 * H + SINK
MASKED = -(2.0 ** 100)
NORM = 2.0 ** 8
KV_SCALE = 2.0 ** -6
LEAST = 2.0 ** -32


def layer_kernel(nc, x, wq, wkv, wku, wvu, wo, wfc, wproj, c_idf, c_idh, c_idb, c_mask0, c_mask1,
                 c_msink, c_bias, c_mov, c_rowlo, c_gmask, c_vsmask, c_vsones, out):
    fp32, fp32r = mybir.dt.float32, mybir.dt.float32r
    bf16, fp16 = mybir.dt.bfloat16, mybir.dt.float16
    ALU = mybir.AluOpType
    ACT = mybir.ActivationFunctionType
    AX = mybir.AxisListType

    ctx = ExitStack()
    with ctx:
        def sb(name, shape, dt):
            return ctx.enter_context(nc.sbuf_tensor(name, shape, dt))

        def sem(name):
            return ctx.enter_context(nc.semaphore(name))

        idf = sb("idf", [P, P], fp32)
        idh = sb("idh", [P, P], fp16)
        idb = sb("idb", [P, P], bf16)
        mask0 = sb("mask0", [P, P], bf16)
        mask1 = sb("mask1", [P, T - BLK], bf16)
        msink = sb("msink", [P, H * SINK], bf16)
        bias = sb("bias", [BIAS_ROWS, 2 * H + 1, P], bf16)
        mov = sb("mov", [BIAS_ROWS, T], bf16)
        rowlo = sb("rowlo", [P, 1], fp32)
        gmask = sb("gmask", [P, G], fp32)
        vsmask = sb("vsmask", [H * SINK, H], fp32)
        ones = sb("ones", [P, P], fp32)
        neghalf = sb("neghalf", [P, 5], fp32)
        wq_r = sb("wq_r", [P, CC, C], fp32)
        wkv_r = sb("wkv_r", [L, C], fp32)
        wku_r = sb("wku_r", [P, CC, L], fp32)
        wvu_r = sb("wvu_r", [P, CC, L], fp32)
        wo_r = sb("wo_r", [P, CC, C], fp32)
        wfc_r = sb("wfc_r", [P, FC, C], fp32)
        wpr_r = sb("wpr_r", [P, CC, F], fp32)
        wqT = sb("wqT", [P, 2, CC, H, 2, HD], fp16)
        wkvT = sb("wkvT", [P, 2, CC, L], fp16)
        wkT = sb("wkT", [L, 2, H, 2, HD], fp16)
        wvT = sb("wvT", [L, 2, C], fp16)
        woT = sb("woT", [P, 2, CC, C], fp16)
        neg_t = sb("neg_t", [P, 2, FC * C], fp16)
        tern = sb("tern", [P, 2, FC * C], fp16)
        fcT = sb("fcT", [P, CC, F], fp16)
        prT = sb("prT", [P, FC, C], fp16)
        wsum = sb("wsum", [P, 2, FC], fp32)
        gam = sb("gam", [P, 2], fp32)
        thr = sb("thr", [P, 2], fp32)
        nthr = sb("nthr", [P, 2], fp32)
        gam128 = sb("gam128", [P, 2], fp32)
        wsq = sb("wsq", [P, 5, 2], fp32)
        junk = sb("junk", [P, 5, CC * C], bf16)
        sq = sb("sq", [P, 5], fp32)
        rsq = sb("rsq", [P, 5], fp32)
        root = sb("root", [P, 5], fp32)
        sc = sb("sc", [P, 5], fp32)
        rr = sb("rr", [P, 2], fp32)
        un = sb("un", [P, 2], fp32)
        xin = sb("xin", [P, TT_, C], fp32)
        st1 = sb("st1", [P, TT_, 6], fp32)
        mv1 = sb("mv1", [P, TT_, 2], fp32)
        ve1 = sb("ve1", [P, TT_], fp32)
        rs1 = sb("rs1", [P, TT_], fp32)
        xn = sb("xn", [P, TT_, C], fp32)
        st2 = sb("st2", [P, TT_, 6], fp32)
        mv2 = sb("mv2", [P, TT_, 2], fp32)
        ve2 = sb("ve2", [P, TT_], fp32)
        rs2 = sb("rs2", [P, TT_], fp32)
        cx = sb("cx", [P, TT_, C], fp32)
        gx = sb("gx", [P, TT_], fp32)
        gxr = sb("gxr", [P, TT_], fp32)
        ga1 = sb("ga1", [P, TT_], fp32)
        a1 = sb("a1", [P, TT_], fp32)
        txs = sb("txs", [P, TT_, C], fp32)
        xhT = sb("xhT", [P, CC, T], fp16)
        xlT = sb("xlT", [P, CC, T], fp16)
        thT = sb("thT", [P, CC, T], fp16)
        tlT = sb("tlT", [P, CC, T], fp16)
        latH = sb("latH", [L, T], fp16)
        latL = sb("latL", [L, T], fp16)
        latSH = sb("latSH", [L, H, SINK], fp16)
        latSL = sb("latSL", [L, H, SINK], fp16)
        qh = sb("qh", [P, NT * T], fp16)
        Q = sb("Q", [P, NT, T], fp16)
        KH = sb("KH", [P, NT, T], fp16)
        KL = sb("KL", [P, NT, T], fp16)
        BDH = sb("BDH", [P, NT, P], fp16)
        BDL = sb("BDL", [P, NT, P], fp16)
        VH = sb("VH", [P, 3, H, VW], fp16)
        VL = sb("VL", [P, 3, H, VW], fp16)
        vs32 = sb("vs32", [H * SINK, H, HD], fp32)
        VSH = sb("VSH", [H * SINK, H, VW], fp16)
        VSL = sb("VSL", [H * SINK, H, VW], fp16)
        mx = sb("mx", [P, TT_, H], fp32)
        smx = sb("smx", [P, TT_, H], fp32)
        mm = sb("mm", [P, TT_, H], fp32)
        mhl = sb("mhl", [P, TT_, 2, H], bf16)
        E32 = sb("E32", [P, 2, 2, 2 * T], fp32)
        EH = sb("EH", [P, G, NT, T], fp16)
        EL = sb("EL", [P, G, NT, T], fp16)
        ES32 = sb("ES32", [H * SINK, T], fp32)
        ESH = sb("ESH", [H * SINK, T], fp16)
        ESL = sb("ESL", [H * SINK, T], fp16)
        rden = sb("rden", [P, TT_, H], fp32)
        y = sb("y", [P, TT_, C], fp32)
        yhT = sb("yhT", [P, CC, T], fp16)
        ylT = sb("ylT", [P, CC, T], fp16)
        xres = sb("xres", [P, TT_, C], fp32)
        xat = sb("xat", [P, TT_, C], fp32)
        ob = sb("ob", [P, TT_, C], fp32)
        gl = sb("gl", [P, TT_, F], fp32)
        sth = sb("sth", [P, TT_, 2, 6], fp32)
        mvh = sb("mvh", [P, TT_, 2], fp32)
        veh = sb("veh", [P, TT_], fp32)
        rsh = sb("rsh", [P, TT_], fp32)
        ch = sb("ch", [P, TT_, F], fp32)
        t2s = sb("t2s", [P, TT_, F], fp32)
        gh = sb("gh", [P, TT_], fp32)
        ghr = sb("ghr", [P, TT_], fp32)
        ga2 = sb("ga2", [P, TT_], fp32)
        a2 = sb("a2", [P, TT_], fp32)
        t2h = sb("t2h", [P, TT_, FC, P], fp16)
        t2l = sb("t2l", [P, TT_, FC, P], fp16)

        ring = [ctx.enter_context(nc.psum_tensor(f"ring{i}", [P, 2, 512], fp32)) for i in range(3)]
        aux = ctx.enter_context(nc.psum_tensor("aux", [P, 512], fp32))
        acc = ctx.enter_context(nc.psum_tensor("acc", [P, 512], fp32))

        def stage(name, per):
            return sem(name), per, 0

        primed = []

        def primed_stage(name, per):
            primed.append(sem(name))
            return primed[-1], per, 1

        ld_id = sem("ld_id"); ld_const = sem("ld_const"); ld_w = [sem(f"ld_w{n}") for n in ("q", "kv", "ku", "vu", "o")]; ld_wf = sem("ld_wf"); ld_wp = sem("ld_wp")
        ld_x = stage("ld_x", 16); ld_res = stage("ld_res", 16); st_out = primed_stage("st_out", 16)
        memsets = sem("memsets")
        N_SET = 8
        N_CONST = 16 * 11
        passed = sem("passed")
        w_tr = sem("w_tr"); w_ev = sem("w_ev"); w_sq = sem("w_sq"); w_lo = sem("w_lo"); w_sqtot = sem("w_sqtot"); bounds = sem("bounds"); roots = sem("roots"); scales = sem("scales"); undo = sem("undo"); w_abs = sem("w_abs"); w_tot = sem("w_tot"); w_tern = sem("w_tern")
        dve_pro = sem("dve_pro"); means = sem("means")
        pool_pro = sem("pool_pro")
        tr_x = stage("tr_x", 1); mm_lat = stage("mm_lat", 1); mm_q = stage("mm_q", 1)
        mm_k = stage("mm_k", 1); mm_v = stage("mm_v", 1);
        xh_ok = stage("xh_ok", 1); xl_ok = stage("xl_ok", 1); th_ok = stage("th_ok", 1); tl_ok = stage("tl_ok", 1)
        lath_ok = stage("lath_ok", 2); latl_ok = stage("latl_ok", 2); qh_ok = stage("qh_ok", 1); q_ok = stage("q_ok", 1)
        kh_ok = stage("kh_ok", 1); kl_ok = stage("kl_ok", 1); bd_ok = stage("bd_ok", 2)
        vh_ok = stage("vh_ok", 1); v_ok = stage("v_ok", 1); vs_ok = stage("vs_ok", 3)
        var1 = stage("var1", TT_); rstd1 = stage("rstd1", 1); xn_ok = stage("xn_ok", TT_)
        gx_ok = stage("gx_ok", TT_); tx_ok = stage("tx_ok", TT_); a1_ok = stage("a1_ok", 1)
        pool_f = stage("pool_f", 4)
        s1 = stage("s1", 6); red1 = stage("red1", 6); red1s = stage("red1s", 1)
        mm_ok = stage("mm_ok", 1); m_ok = stage("m_ok", 2); mT = stage("mT", 1); mT_ok = stage("mT_ok", 1)
        s2 = stage("s2", 4); s2s = primed_stage("s2s", 1); ex = primed_stage("ex", 4); exh = stage("exh", 4); el_ok = primed_stage("el_ok", 4); exs = stage("exs", 2); els = stage("els", 1)
        pv = primed_stage("pv", TT_); y_ok = stage("y_ok", TT_); tr_y = primed_stage("tr_y", 1)
        yh_ok = stage("yh_ok", 1); yl_ok = stage("yl_ok", 1); mm_wo = primed_stage("mm_wo", 1)
        fc = stage("fc", TT_); gelu = primed_stage("gelu", TT_); ch_ok = stage("ch_ok", TT_); t2 = primed_stage("t2", TT_); gh_ok = stage("gh_ok", TT_)
        tr_h = stage("tr_h", TT_); t2h_ok = stage("t2h_ok", TT_); t2l_ok = primed_stage("t2l_ok", TT_)
        pr = primed_stage("pr", TT_); a2_ok = primed_stage("a2_ok", TT_); pool_b = stage("pool_b", 6)
        xa_ok = primed_stage("xa_ok", TT_); o_ok = primed_stage("o_ok", TT_)
        DF, DB = 9, 10
        dve_f = stage("dve_f", DF); dve_b = stage("dve_b", DB)

        def wait(eng, st, b, k=None):
            s, per, start = st
            v = b * per + (per if k is None else k) + start
            if not isinstance(v, int) or v > start:
                eng.wait_ge(s, v)

        def wait_before(eng, st, b):
            wait(eng, st, b, 0)

        def wait_apart(eng, st, b, k=None):
            wait(eng, st, b, k)
            if not isinstance(b, int):
                eng.sem_inc(passed, 1)

        x_v = x.rearrange("b (i p) c -> b p i c", p=P)
        out_v = out.rearrange("b (i p) c -> b p i c", p=P)

        USES = (
            [("fc", i, [(gelu, i + 1)]) for i in range(TT_)]
            + [("f_tr", 0, [(xl_ok, 1), (tl_ok, 1)])]
            + [("p2", r, [(exh, r + 1)]) for r in range(4)]
            + [("f_q", 0, [(q_ok, 1)]), ("f_k", 0, [(kl_ok, 1)])]
            + [("t2T", i, [(t2l_ok, i + 1)]) for i in range(TT_)]
            + [("f_v", 0, [(v_ok, 1), (vs_ok, 1)])]
            + [("f_p1", r, [(red1, r + 1)] + ([(red1s, 1)] if r == 5 else [])) for r in range(6)]
        )
        NU = len(USES)
        assert NU % 3 == 0
        AT = {(n, i): u for u, (n, i, _) in enumerate(USES)}

        def take(eng, name, i, b, back, front):
            u = AT[(name, i)]
            v, cur = u, True
            while True:
                v -= 3
                if v < 0:
                    v += NU
                    if not cur:
                        break
                    cur = False
                is_front = USES[v][0].startswith("f_")
                if cur and not (front if is_front else back):
                    continue
                if not cur and not is_front and not back:
                    continue
                if not cur and is_front and not back:
                    break
                for st, k in USES[v][2]:
                    if cur:
                        wait(eng, st, b + 1 if is_front else b, k)
                    elif is_front:
                        wait(eng, st, b, k)
                    else:
                        wait_before(eng, st, b)
                break
            return ring[u % 3]

        def schedule(eng, body):
            body(-2, False, False, True)
            body(-1, False, True, True)
            with eng.Fori(0, B - 2) as b:
                body(b, True, True, True)
            body(B - 2, True, True, False)
            body(B - 1, True, False, False)

        block = ctx.enter_context(nc.Block())

        @block.sync
        def _(sp):
            sp.dma_start(idf[:], c_idf).then_inc(ld_id, 16)
            sp.dma_start(xin[:], x_v[0]).then_inc(ld_x[0], 16)
            sp.dma_start(wfc_r[:], wfc.rearrange("(c p) k -> p c k", p=P)).then_inc(ld_wf, 16)
            sp.dma_start(wpr_r[:], wproj.rearrange("(c p) k -> p c k", p=P)).then_inc(ld_wp, 16)
            for dst, src in ((rowlo, c_rowlo), (gmask, c_gmask), (vsmask, c_vsmask), (idh, c_idh), (VSH, c_vsones),
                             (idb, c_idb), (mask0, c_mask0), (mask1, c_mask1), (msink, c_msink), (mov, c_mov),
                             (bias, c_bias)):
                view = dst[:].bitcast(mybir.dt.uint16) if dst.dtype == bf16 else dst[:]
                sp.dma_start(view, src).then_inc(ld_const, 16)

            def body(b, back, front, rows):
                if back:
                    wait_before(sp, xa_ok, b)
                    sp.dma_start(xres[:], x_v[b]).then_inc(ld_res[0], 16)
                    wait(sp, o_ok, b)
                    sp.dma_start(out_v[b], ob[:]).then_inc(st_out[0], 16)

            schedule(sp, body)
            wait(sp, st_out, B - 1)

        @block.gpsimd
        def _(pool):
            for n, (dst, v) in enumerate(((neghalf, -0.5), (wsq, 0.0), (ones, 1.0), (BDH, 0.0), (BDL, 0.0),
                                          (VH, 1.0), (VL, 0.0), (VSL, 0.0))):
                nc.gpsimd.memset(dst[:], v).then_inc(memsets, 1)
            pool.wait_ge(memsets, N_SET)
            for s in primed:
                pool.sem_inc(s, 1)

            def norms():
                pool.wait_ge(bounds, 1)
                nc.gpsimd.tensor_tensor(rsq[:], sq[:], neghalf[:], ALU.pow).then_inc(pool_pro, 1)
                pool.wait_ge(pool_pro, 1)
                nc.gpsimd.tensor_tensor(root[:], sq[:], rsq[:], ALU.mult).then_inc(roots, 1)

            def low_half(b, r):
                gp, tp = divmod(r, 2)
                wait(pool, ex, b, r + 1)
                wait(pool, exh, b, r + 1)
                if r == 0:
                    wait_before(pool, pv, b)
                at = (slice(None), slice(2 * gp, 2 * gp + 2), slice(2 * tp, 2 * tp + 2))
                nc.gpsimd.tensor_tensor(EL[at].rearrange("p g t q -> p g (t q)"), E32[:, r % 2],
                                        EH[at].rearrange("p g t q -> p g (t q)"), ALU.subtract).then_inc(el_ok[0], 1)

            def body(b, back, front, rows):
                n = b + 2
                if back:
                    low_half(b, 0)
                if rows:
                    wait_apart(pool, var1, n)
                    nc.gpsimd.tensor_scalar(ve1[:], mv1[:, :, 1], LN_EPS, None, ALU.add).then_inc(pool_f[0], 1)
                    wait(pool, pool_f, n, 1)
                    nc.gpsimd.tensor_tensor(rs1[:], ve1[:], neghalf[:, 0:TT_], ALU.pow).then_inc(rstd1[0], 1)
                if back:
                    for r in range(1, 4):
                        low_half(b, r)
                    wait(pool, exs, b)
                    nc.gpsimd.tensor_tensor(ESL[:], ES32[:], ESH[:], ALU.subtract).then_inc(els[0], 1)
                if front:
                    if back:
                        wait(pool, gelu, b)
                    else:
                        pool.wait_ge(means, 1)
                    wait_apart(pool, pool_f, b + 1, 4)
                    nc.gpsimd.tensor_scalar(a1[:], ga1[:], gam128[:, 0:1], None, ALU.mult).then_inc(a1_ok[0], 1)
                if back:
                    for i in range(TT_):
                        wait_apart(pool, gh_ok, b, i + 1)
                        nc.gpsimd.tensor_scalar(veh[:, i:i + 1], mvh[:, i, 1:2], FFN_EPS, None, ALU.add).then_inc(pool_b[0], 1)
                        wait(pool, pool_b, b, 3 * i + 1)
                        nc.gpsimd.tensor_tensor(rsh[:, i:i + 1], veh[:, i:i + 1], neghalf[:, 0:1], ALU.pow).then_inc(pool_b[0], 1)
                        wait(pool, pool_b, b, 3 * i + 2)
                        nc.gpsimd.tensor_tensor(ga2[:, i:i + 1], rsh[:, i:i + 1], gh[:, i:i + 1], ALU.mult).then_inc(pool_b[0], 1)
                        if i == 0:
                            wait_before(pool, o_ok, b)
                        wait_apart(pool, pool_b, b, 3 * i + 3)
                        nc.gpsimd.tensor_scalar(a2[:, i:i + 1], ga2[:, i:i + 1], gam128[:, 1:2], None, ALU.mult).then_inc(a2_ok[0], 1)
                if rows:
                    wait_apart(pool, gx_ok, n)
                    nc.gpsimd.tensor_scalar(ve2[:], mv2[:, :, 1], FFN_EPS, None, ALU.add).then_inc(pool_f[0], 1)
                    wait(pool, pool_f, n, 2)
                    nc.gpsimd.tensor_tensor(rs2[:], ve2[:], neghalf[:, 0:TT_], ALU.pow).then_inc(pool_f[0], 1)
                    wait(pool, pool_f, n, 3)
                    if front:
                        wait(pool, a1_ok, n - 1)
                    nc.gpsimd.tensor_tensor(ga1[:], rs2[:], gx[:], ALU.mult).then_inc(pool_f[0], 1)
                if not (back or front):
                    norms()

            schedule(pool, body)

        @block.scalar
        def _(act):
            for n, (dst, src) in enumerate(((wq_r[:], wq.rearrange("(c p) k -> p c k", p=P)), (wkv_r[:], wkv),
                                            (wku_r[:], wku.rearrange("(c p) k -> p c k", p=P)),
                                            (wvu_r[:], wvu.rearrange("(c p) k -> p c k", p=P)),
                                            (wo_r[:], wo.rearrange("(c p) k -> p c k", p=P)))):
                act.dma_start(dst, src).then_inc(ld_w[n], 16)

            for n, w in enumerate((wq_r, wkv_r, wku_r, wvu_r, wo_r)):
                act.wait_ge(ld_w[n], 16)
                if n == 0:
                    act.wait_ge(memsets, N_SET)
                rows = w.shape[0]
                flat = w[:].rearrange("p a k -> p (a k)") if len(w.shape) == 3 else w[:]
                nc.scalar.activation(junk[0:rows, n, 0:flat.shape[1]], flat, ACT.Square, accum_out=wsq[0:rows, n, 0:1]).then_inc(w_sq, 1)

            act.wait_ge(w_tr, 1)
            act.wait_ge(scales, 1)
            for c in range(CC):
                nc.scalar.activation(wqT[:, 0, c, :, :, :], ring[0][:, c, 0:C].rearrange("p (h e) -> p h e", h=H).unsqueeze(2).to_broadcast([P, H, 2, HD]),
                                     ACT.Copy, scale=sc[:, 0:1]).then_inc(w_ev, 1)
            act.wait_ge(w_tr, 2)
            nc.scalar.activation(wkvT[:, 0], ring[1][:, 0, 0:CC * L].rearrange("p (c l) -> p c l", c=CC), ACT.Copy, scale=sc[:, 1:2]).then_inc(w_ev, 1)
            nc.scalar.activation(wkT[:, 0], ring[1][0:L, 1, 0:C].rearrange("p (h e) -> p h e", h=H).unsqueeze(2).to_broadcast([L, H, 2, HD]),
                                 ACT.Copy, scale=sc[0:L, 2:3]).then_inc(w_ev, 1)
            nc.scalar.activation(wvT[:, 0], ring[1][0:L, 1, C:2 * C], ACT.Copy, scale=sc[0:L, 3:4]).then_inc(w_ev, 1)
            act.wait_ge(w_tr, 3)
            nc.scalar.activation(woT[:, 0], ring[2][:, :, 0:C], ACT.Copy, scale=sc[:, 4:5]).then_inc(w_ev, 1)

            def body(b, back, front, rows):
                f = b + 1
                def exponentials(r):
                    gp, tp = divmod(r, 2)
                    at = (slice(None), slice(2 * gp, 2 * gp + 2), slice(2 * tp, 2 * tp + 2))
                    src = ring[AT[("p2", r)] % 3]
                    wait(act, s2, b, r + 1)
                    if r < 2:
                        wait_before(act, el_ok, b)
                    else:
                        wait(act, el_ok, b, r - 1)
                    nc.scalar.activation(E32[:, r % 2], src[:], ACT.Exp, scale=un[:, 0:1]).then_inc(ex[0], 1)
                    nc.scalar.activation(EH[at].rearrange("p g t q -> p g (t q)"), src[:], ACT.Exp, scale=un[:, 0:1]).then_inc(exh[0], 1)

                if front and rows:
                    wait(act, xn_ok, b + 1)
                    act.dma_start(xin[:], x_v[b + 2]).then_inc(ld_x[0], 16)
                if back:
                    for i in range(TT_):
                        wait(act, fc, b, i + 1)
                        if i == 0:
                            wait(act, a1_ok, b)
                            wait_before(act, t2, b)
                        nc.scalar.activation(gl[:, i, :], ring[AT[("fc", i)] % 3][:].rearrange("p a n -> p (a n)"),
                                             ACT.Gelu, scale=a1[:, i:i + 1]).then_inc(gelu[0], 1)
                if front:
                    wait(act, tr_x, f)
                    src = ring[AT[("f_tr", 0)] % 3]
                    if back:
                        wait(act, mm_q, b)
                    nc.scalar.activation(xhT[:], src[:, 0, :].rearrange("p (c t) -> p c t", c=CC), ACT.Copy).then_inc(xh_ok[0], 1)
                    if back:
                        wait(act, fc, b)
                    nc.scalar.activation(thT[:], src[:, 1, :].rearrange("p (c t) -> p c t", c=CC), ACT.Copy).then_inc(th_ok[0], 1)
                    if not back:
                        weights()
                if back:
                    wait(act, s2s, b)
                    wait_before(act, pv, b)
                    for e in (ES32, ESH):
                        nc.scalar.activation(e[:], aux[0:H * SINK, 0:T], ACT.Exp, scale=un[0:H * SINK, 0:1]).then_inc(exs[0], 1)
                    exponentials(0)
                    exponentials(1)
                if front:
                    wait(act, mm_lat, f)
                    if back:
                        wait(act, mm_v, b)
                    nc.scalar.activation(latH[:], aux[0:L, 0:T], ACT.Copy).then_inc(lath_ok[0], 1)
                    nc.scalar.activation(latSH[:], aux[0:L, 0:SINK].unsqueeze(1).to_broadcast([L, H, SINK]),
                                         ACT.Copy).then_inc(lath_ok[0], 1)
                if back:
                    exponentials(2)
                    exponentials(3)
                if front:
                    wait(act, mm_q, f)
                    if back:
                        wait(act, q_ok, b)
                    nc.scalar.activation(qh[:], ring[AT[("f_q", 0)] % 3][:].rearrange("p a n -> p (a n)"), ACT.Copy).then_inc(qh_ok[0], 1)
                    wait(act, mm_k, f)
                    if back:
                        wait(act, s2s, b)
                    nc.scalar.activation(KH[:].rearrange("p t n -> p (t n)"), ring[AT[("f_k", 0)] % 3][:].rearrange("p a n -> p (a n)"),
                                         ACT.Copy, scale=KV_SCALE).then_inc(kh_ok[0], 1)
                if back:
                    for i in range(TT_):
                        wait(act, tr_h, b, i + 1)
                        if i == 0:
                            wait_before(act, pr, b)
                        nc.scalar.activation(t2h[:, i].rearrange("p k n -> p (k n)"), ring[AT[("t2T", i)] % 3][:].rearrange("p a n -> p (a n)"),
                                             ACT.Copy).then_inc(t2h_ok[0], 1)
                if front:
                    wait(act, mm_v, f)
                    if back:
                        wait(act, pv, b)
                    else:
                        act.wait_ge(memsets, N_SET)
                    slot = ring[AT[("f_v", 0)] % 3]
                    nc.scalar.activation(VH[:, :, :, 0:HD], slot[:].rearrange("p a n -> p (a n)")[:, 0:3 * C]
                                         .rearrange("p (j h d) -> p j h d", j=3, h=H), ACT.Copy, scale=KV_SCALE).then_inc(vh_ok[0], 1)
                    if not back:
                        weights_transposed()
                if back:
                    wait(act, tr_y, b)
                    wait_before(act, mm_wo, b)
                    nc.scalar.activation(yhT[:], aux[:].rearrange("p (c t) -> p c t", c=CC), ACT.Copy).then_inc(yh_ok[0], 1)

            def weights():
                act.wait_ge(ld_wp, 16)
                for c in range(FC):
                    nc.scalar.activation(tern[:, 1, c * C:(c + 1) * C], wpr_r[:, c // 4, (c % 4) * C:(c % 4 + 1) * C], ACT.Abs,
                                         accum_out=wsum[:, 1, c:c + 1]).then_inc(w_abs, 1)

            def weights_transposed():
                for c in range(CC):
                    act.wait_ge(w_tr, 4 + c)
                    nc.scalar.activation(fcT[:, c, :], ring[c][:, 0, :].bitcast(fp16), ACT.Copy).then_inc(w_ev, 1)

            schedule(act, body)

        @block.vector
        def _(dve):
            def flat(t):
                return t.rearrange("p a n -> p (a n)")

            pro = [0]

            def did_pro(ins):
                pro[0] += 1
                ins.then_inc(dve_pro, 1)

            def settle_pro():
                dve.wait_ge(dve_pro, pro[0])

            def scale_factors():
                dve.wait_ge(w_sqtot, 1)
                nc.vector.tensor_scalar(sq[:], acc[:, 0:10].rearrange("p (a c) -> p a c", a=5)[:, :, 0], LEAST, None, ALU.max).then_inc(bounds, 1)
                dve.wait_ge(roots, 1)
                nc.vector.tensor_scalar(sc[:], rsq[:], NORM, None, ALU.mult).then_inc(scales, 1)
                did_pro(nc.vector.tensor_scalar(rr[:, 0:1], root[:, 0:1], root[:, 2:3], 1.0 / (NORM ** 2 * HD ** 0.5), ALU.mult, ALU.mult))
                did_pro(nc.vector.tensor_scalar(rr[:, 1:2], root[:, 4:5], root[:, 3:4], NORM ** -2, ALU.mult, ALU.mult))
                settle_pro()
                nc.vector.tensor_scalar(un[:], rr[:], root[:, 1:2], 1.0 / (NORM * KV_SCALE), ALU.mult, ALU.mult).then_inc(undo, 1)

            def weight_low_halves():
                def low(ev, k, lo, src, hi):
                    dve.wait_ge(w_ev, ev)
                    nc.vector.scalar_tensor_tensor(out=lo, in0=src, scalar=sc[0:src.shape[0], k:k + 1], in1=hi,
                                                   op0=ALU.mult, op1=ALU.subtract).then_inc(w_lo, 1)

                for c in range(CC):
                    for d in range(2):
                        low(1 + c, 0, wqT[:, 1, c, :, d, :], ring[0][:, c, 0:C].rearrange("p (h e) -> p h e", h=H), wqT[:, 0, c, :, d, :])
                low(3, 1, wkvT[:, 1], ring[1][:, 0, 0:CC * L].rearrange("p (c l) -> p c l", c=CC), wkvT[:, 0])
                for d in range(2):
                    low(5, 2, wkT[:, 1, :, d, :], ring[1][0:L, 1, 0:C].rearrange("p (h e) -> p h e", h=H), wkT[:, 0, :, d, :])
                low(5, 3, wvT[:, 1], ring[1][0:L, 1, C:2 * C], wvT[:, 0])
                low(6, 4, woT[:, 1], ring[2][:, :, 0:C], woT[:, 0])

            def weight_sums():
                dve.wait_ge(ld_wf, 16)
                nc.vector.tensor_reduce(out=wsum[:, 0, :], in_=wfc_r[:], axis=AX.X, op=ALU.add,
                                        apply_absolute_value=True).then_inc(w_abs, 1)

            def weights():
                dve.wait_ge(w_tot, 1)
                did_pro(nc.vector.tensor_reduce(out=gam[:], in_=acc[:, 0:2 * FC].rearrange("p (a c) -> p a c", a=2), axis=AX.X, op=ALU.add))
                settle_pro()
                nc.vector.tensor_scalar(gam128[:], gam[:], 1.0 / (F * C * QB), None, ALU.mult).then_inc(means, 1)
                did_pro(nc.vector.tensor_scalar(thr[:], gam[:], 1.0 / (F * C), FFN_EPS, ALU.mult, ALU.add))
                settle_pro()
                did_pro(nc.vector.tensor_scalar(nthr[:], thr[:], -0.5, None, ALU.mult))
                did_pro(nc.vector.tensor_scalar(thr[:], thr[:], 0.5, None, ALU.mult))
                settle_pro()

            def ternary(n):
                w = flat((wfc_r, wpr_r)[n])
                did_pro(nc.vector.tensor_scalar(neg_t[:, n], w, nthr[:, n:n + 1], None, ALU.is_lt))
                settle_pro()
                nc.vector.scalar_tensor_tensor(out=tern[:, n], in0=w, scalar=thr[:, n:n + 1], in1=neg_t[:, n],
                                               op0=ALU.is_gt, op1=ALU.subtract).then_inc(w_tern, 1)

            def second_transposed():
                for j, slot in enumerate((acc, aux)):
                    dve.wait_ge(w_tr, 6 + j)
                    nc.vector.tensor_copy(prT[:, 4 * j:4 * j + 4, :], slot[:].bitcast(fp16).rearrange("p (k c) -> p k c", k=4)).then_inc(w_ev, 1)

            def body(b, back, front, rows):
                f = b + 1
                steps = {"f": 0, "b": 0}

                def did(ins, w):
                    steps[w] += 1
                    ins.then_inc((dve_f if w == "f" else dve_b)[0], 1)

                def settle(w, how=wait):
                    how(dve, dve_f if w == "f" else dve_b, b + 2 if w == "f" else b, steps[w])

                def maxima(r):
                    wait(dve, s1, f, r + 1)
                    src = ring[AT[("f_p1", r)] % 3]
                    if r < 2:
                        nc.vector.tensor_reduce(out=mx[:, 0, 8 * r:8 * r + 8], in_=src[:].rearrange("p a (t k) -> p (a t) k", t=NT),
                                                axis=AX.X, op=ALU.max).then_inc(red1[0], 1)
                    else:
                        gp, tp = divmod(r - 2, 2)
                        o = mx[:, 1, :].rearrange("p (g t) -> p g t", g=G)[:, 2 * gp:2 * gp + 2, 2 * tp:2 * tp + 2]
                        nc.vector.tensor_reduce(out=o, in_=src[:, :, 0:2 * (T - BLK)].rearrange("p a (t k) -> p a t k", t=2),
                                                axis=AX.X, op=ALU.max).then_inc(red1[0], 1)

                n = b + 2

                def row_stats():
                    wait(dve, ld_x, n)
                    for i in range(TT_):
                        did(nc.vector.bn_stats(st1[:, i, :], xin[:, i, :]), "f")
                    settle("f", wait_apart)
                    for i in range(TT_):
                        nc.vector.bn_aggr(mv1[:, i, :], st1[:, i, :]).then_inc(var1[0], 1)

                def row_norm():
                    wait(dve, rstd1, n)
                    wait(dve, var1, n)
                    if front:
                        wait(dve, tr_x, b + 1)
                    for i in range(TT_):
                        nc.vector.tensor_scalar(xn[:, i, :], xin[:, i, :], mv1[:, i, 0:1], rs1[:, i:i + 1],
                                                ALU.subtract, ALU.mult).then_inc(xn_ok[0], 1)
                    wait(dve, xn_ok, n)
                    for i in range(TT_):
                        did(nc.vector.bn_stats(st2[:, i, :], xn[:, i, :]), "f")
                    settle("f", wait_apart)
                    for i in range(TT_):
                        did(nc.vector.bn_aggr(mv2[:, i, :], st2[:, i, :]), "f")
                    settle("f")

                def row_scale():
                    for i in range(TT_):
                        did(nc.vector.tensor_scalar(cx[:, i, :], xn[:, i, :], mv2[:, i, 0:1], None, ALU.subtract), "f")
                    settle("f")
                    if front:
                        wait(dve, pool_f, b + 1)
                    for i in range(TT_):
                        nc.vector.tensor_reduce(out=gx[:, i:i + 1], in_=cx[:, i, :], axis=AX.X, op=ALU.max,
                                                apply_absolute_value=True).then_inc(gx_ok[0], 1)
                    wait(dve, gx_ok, n)
                    did(nc.vector.reciprocal(gxr[:], gx[:]), "f")
                    settle("f")
                    for i in range(TT_):
                        nc.vector.tensor_scalar(txs[:, i, :], cx[:, i, :], gxr[:, i:i + 1], QB, ALU.mult, ALU.mult).then_inc(tx_ok[0], 1)

                if back:
                    wait(dve, mT, b)
                    wait_before(dve, s2s, b)
                    nc.vector.tensor_copy(mov[BLK:BLK + 2 * H, :], aux[BLK:BLK + 2 * H, 0:T // 2].bitcast(bf16)).then_inc(mT_ok[0], 1)
                if not (back or front):
                    row_stats()
                    row_norm()
                    row_scale()
                    scale_factors()
                    weight_low_halves()
                    weight_sums()

                def hidden_centred(i):
                    wait(dve, gelu, b, i + 1)
                    for j in range(2):
                        did(nc.vector.bn_stats(sth[:, i, j, :], gl[:, i, 512 * j:512 * j + 512]), "b")
                    settle("b", wait_apart)
                    did(nc.vector.bn_aggr(mvh[:, i, :], flat(sth[:, i])), "b")
                    settle("b")
                    nc.vector.tensor_scalar(ch[:, i, :], gl[:, i, :], mvh[:, i, 0:1], None, ALU.subtract).then_inc(ch_ok[0], 1)

                def hidden_scaled(i):
                    wait(dve, ch_ok, b, i + 1)
                    if i == 0:
                        wait_before(dve, a2_ok, b)
                    nc.vector.tensor_reduce(out=gh[:, i:i + 1], in_=ch[:, i, :], axis=AX.X, op=ALU.max,
                                            apply_absolute_value=True).then_inc(gh_ok[0], 1)
                    wait(dve, gh_ok, b, i + 1)
                    did(nc.vector.reciprocal(ghr[:, i:i + 1], gh[:, i:i + 1]), "b")
                    settle("b")
                    nc.vector.tensor_scalar(t2s[:, i, :], ch[:, i, :], ghr[:, i:i + 1], QB, ALU.mult, ALU.mult).then_inc(t2[0], 1)

                def hidden_low(i):
                    wait(dve, t2h_ok, b, i + 1)
                    nc.vector.tensor_tensor(t2l[:, i].rearrange("p k n -> p (k n)"), ring[AT[("t2T", i)] % 3][:].rearrange("p a n -> p (a n)"),
                                            t2h[:, i].rearrange("p k n -> p (k n)"), ALU.subtract).then_inc(t2l_ok[0], 1)

                if back:
                    hidden_centred(0)
                if front:
                    wait(dve, tr_x, f)
                    src = ring[AT[("f_tr", 0)] % 3]
                    wait(dve, xh_ok, f)
                    nc.vector.tensor_tensor(xlT[:], src[:, 0, :].rearrange("p (c t) -> p c t", c=CC), xhT[:], ALU.subtract).then_inc(xl_ok[0], 1)
                    wait(dve, th_ok, f)
                    nc.vector.tensor_tensor(tlT[:], src[:, 1, :].rearrange("p (c t) -> p c t", c=CC), thT[:], ALU.subtract).then_inc(tl_ok[0], 1)
                if back:
                    hidden_scaled(0)
                if rows and (front or back):
                    row_stats()
                if back:
                    hidden_centred(1)
                if front:
                    wait(dve, mm_lat, f)
                    wait(dve, lath_ok, f)
                    nc.vector.tensor_tensor(latL[:], aux[0:L, 0:T], latH[:], ALU.subtract).then_inc(latl_ok[0], 1)
                    nc.vector.tensor_tensor(latSL[:], aux[0:L, 0:SINK].unsqueeze(1).to_broadcast([L, H, SINK]), latSH[:], ALU.subtract).then_inc(latl_ok[0], 1)
                if back:
                    hidden_scaled(1)
                if rows and (front or back):
                    row_norm()
                if front:
                    if not back:
                        weights()
                        ternary(0)
                        ternary(1)
                    wait(dve, qh_ok, f)
                    if not back:
                        dve.wait_ge(ld_const, N_CONST)
                        dve.wait_ge(memsets, N_SET)
                    nc.vector.scalar_tensor_tensor(out=flat(Q), in0=qh[:], scalar=rowlo[:, 0:1],
                                                   in1=ring[AT[("f_q", 0)] % 3][:].rearrange("p a n -> p (a n)"),
                                                   op0=ALU.mult, op1=ALU.add).then_inc(q_ok[0], 1)
                    wait(dve, kh_ok, f)
                    nc.vector.scalar_tensor_tensor(out=flat(KL), in0=ring[AT[("f_k", 0)] % 3][:].rearrange("p a n -> p (a n)"), scalar=KV_SCALE,
                                                   in1=flat(KH), op0=ALU.mult, op1=ALU.subtract).then_inc(kl_ok[0], 1)
                    wait(dve, kl_ok, f)
                    for d, s in ((BDH, KH), (BDL, KL)):
                        o = flat(d).rearrange("p (t n) -> p t n", t=NT)
                        o = bass.AP(o.tensor, o.offset, [o.ap[0], [P + SINK, NT], [NT * SINK, G], [1, SINK]])
                        nc.vector.tensor_tensor(o, s[:, :, 0:SINK].unsqueeze(2).to_broadcast([P, NT, G, SINK]),
                                                gmask[:].unsqueeze(1).unsqueeze(3).to_broadcast([P, NT, G, SINK]), ALU.mult).then_inc(bd_ok[0], 1)
                if back:
                    hidden_low(0)
                if back:
                    for i in range(TT_):
                        wait(dve, pv, b, i + 1)
                        o = (acc if i == 0 else aux)[:, 0:H * VW].rearrange("p (h d) -> p h d", h=H)
                        did(nc.vector.reciprocal(rden[:, i, :], o[:, :, HD]), "b")
                        settle("b")
                        if i == 0:
                            wait_before(dve, tr_y, b)
                        nc.vector.tensor_tensor(y[:, i, :].rearrange("p (h d) -> p h d", h=H), o[:, :, 0:HD],
                                                rden[:, i, :].unsqueeze(2).to_broadcast([P, H, HD]), ALU.mult).then_inc(y_ok[0], 1)
                if back:
                    hidden_low(1)
                if front:
                    wait(dve, vh_ok, f)
                    nc.vector.scalar_tensor_tensor(out=VL[:, :, :, 0:HD], in0=ring[AT[("f_v", 0)] % 3][:].rearrange("p a n -> p (a n)")[:, 0:3 * C]
                                                   .rearrange("p (j h d) -> p j h d", j=3, h=H), scalar=KV_SCALE, in1=VH[:, :, :, 0:HD],
                                                   op0=ALU.mult, op1=ALU.subtract).then_inc(v_ok[0], 1)
                    wait(dve, mm_v, f)
                    nc.vector.scalar_tensor_tensor(out=vs32[:], in0=ring[AT[("f_v", 0)] % 3][0:H * SINK, 1, C:2 * C].rearrange("p (h d) -> p h d", h=H), scalar=KV_SCALE,
                                                   in1=vsmask[:].unsqueeze(2).to_broadcast([H * SINK, H, HD]), op0=ALU.mult, op1=ALU.mult).then_inc(vs_ok[0], 1)
                if back:
                    wait(dve, yh_ok, b)
                    wait_before(dve, mm_wo, b)
                    nc.vector.tensor_tensor(ylT[:], aux[:].rearrange("p (c t) -> p c t", c=CC), yhT[:], ALU.subtract).then_inc(yl_ok[0], 1)
                if rows and (front or back):
                    row_scale()
                if front:
                    for r in range(3):
                        maxima(r)
                if back:
                    wait(dve, mm_wo, b)
                    wait(dve, ld_res, b)
                    for i in range(TT_):
                        nc.vector.scalar_tensor_tensor(out=xat[:, i, :], in0=aux[:, i * C:(i + 1) * C], scalar=un[:, 1:2],
                                                       in1=xres[:, i, :], op0=ALU.mult, op1=ALU.add).then_inc(xa_ok[0], 1)
                if front:
                    for r in range(3, 6):
                        maxima(r)
                    nc.vector.tensor_reduce(out=flat(smx), in_=ring[AT[("f_p1", 5)] % 3][:, 0, 512 - TT_ * H * SINK:512].rearrange("p (h s) -> p h s", s=SINK),
                                            axis=AX.X, op=ALU.max).then_inc(red1s[0], 1)
                    wait(dve, red1, f)
                    wait(dve, red1s, f)
                    nc.vector.tensor_tensor(flat(mm), flat(mx), flat(smx), ALU.max).then_inc(mm_ok[0], 1)
                    wait(dve, mm_ok, f)
                    if back:
                        wait(dve, mT, b)
                    nc.vector.tensor_scalar(mhl[:, :, 0, :], mm[:], -1.0, None, ALU.mult).then_inc(m_ok[0], 1)
                    wait(dve, m_ok, f, 1)
                    nc.vector.scalar_tensor_tensor(out=mhl[:, :, 1, :], in0=mm[:], scalar=-1.0, in1=mhl[:, :, 0, :],
                                                   op0=ALU.mult, op1=ALU.subtract).then_inc(m_ok[0], 1)
                if back:
                    wait(dve, xa_ok, b)
                    wait_before(dve, st_out, b)
                    for i in range(TT_):
                        wait(dve, pr, b, i + 1)
                        wait(dve, a2_ok, b, i + 1)
                        nc.vector.scalar_tensor_tensor(out=ob[:, i, :], in0=acc[:, i * C:(i + 1) * C], scalar=a2[:, i:i + 1],
                                                       in1=xat[:, i, :], op0=ALU.mult, op1=ALU.add).then_inc(o_ok[0], 1)
                if front:
                    wait(dve, vs_ok, f, 1)
                    nc.vector.tensor_copy(VSH[:, :, 0:HD], vs32[:]).then_inc(vs_ok[0], 1)
                    wait(dve, vs_ok, f, 2)
                    nc.vector.tensor_tensor(VSL[:, :, 0:HD], vs32[:], VSH[:, :, 0:HD], ALU.subtract).then_inc(vs_ok[0], 1)
                if front and not back:
                    second_transposed()
                assert not rows or steps["f"] == DF, steps
                assert not back or steps["b"] == DB, steps

            schedule(dve, body)

        @block.tensor
        def _(pe):
            def flat(t):
                return t.rearrange("p a n -> p (a n)")

            pe.wait_ge(ld_id, 16)
            pe.wait_ge(ld_w[0], 16)
            for c in range(CC):
                for r in range(CC):
                    last = nc.tensor.transpose(ring[0][:, c, r * P:(r + 1) * P], wq_r[:, r, c * P:(c + 1) * P], idf[:])
            last.then_inc(w_tr, 1)
            pe.wait_ge(ld_w[1], 16)
            for c in range(CC):
                nc.tensor.transpose(ring[1][:, 0, c * L:(c + 1) * L], wkv_r[:, c * P:(c + 1) * P], idf[0:L, 0:L])
            for n, w in enumerate((wku_r, wvu_r)):
                pe.wait_ge(ld_w[2 + n], 16)
                for r in range(CC):
                    last = nc.tensor.transpose(ring[1][0:L, 1, n * C + r * P:n * C + (r + 1) * P], w[:, r, :], idf[:])
            last.then_inc(w_tr, 1)
            pe.wait_ge(ld_w[4], 16)
            for c in range(CC):
                for r in range(CC):
                    last = nc.tensor.transpose(ring[2][:, c, r * P:(r + 1) * P], wo_r[:, r, c * P:(c + 1) * P], idf[:])
            last.then_inc(w_tr, 1)
            pe.wait_ge(w_sq, 5)
            nc.tensor.matmul(acc[:, 0:10], ones[:], flat(wsq), start=True, stop=True).then_inc(w_sqtot, 1)
            N_EV, N_LO = 6, 9
            HALVES = ((0, 0), (0, 1), (1, 0))

            def weight_totals():
                pe.wait_ge(w_abs, 1 + FC)
                pe.wait_ge(bounds, 1)
                nc.tensor.matmul(acc[:, 0:2 * FC], ones[:], flat(wsum), start=True, stop=True).then_inc(w_tot, 1)

            def weights():
                wait(pe, red1, 0)
                pe.wait_ge(w_tern, 1)
                for c in range(CC):
                    for k in range(FC):
                        last = nc.tensor.transpose(ring[c][:, 0, :].bitcast(fp16)[:, k * P:(k + 1) * P],
                                                   tern[:, 0, k * C + c * P:k * C + (c + 1) * P], idh[:])
                    last.then_inc(w_tr, 1)
                pe.wait_ge(w_tern, 2)
                pe.wait_ge(means, 1)
                for j, slot in enumerate((acc, aux)):
                    for k in range(4):
                        for c in range(CC):
                            last = nc.tensor.transpose(slot[:].bitcast(fp16)[:, k * C + c * P:k * C + (c + 1) * P],
                                                       tern[:, 1, c * F + (4 * j + k) * P:c * F + (4 * j + k + 1) * P], idh[:])
                    last.then_inc(w_tr, 1)
                pe.wait_ge(w_ev, N_EV + 4)

            def body(b, back, front, rows):
                f = b + 1

                def slot(name, i=0):
                    return take(pe, name, i, b, back, front)

                def fc_tile(i):
                    if i == 0:
                        wait(pe, th_ok, b); wait(pe, tl_ok, b)
                    s = slot("fc", i)
                    for n in range(2):
                        for m, (c, src) in enumerate([(c, src) for src in (thT, tlT) for c in range(CC)]):
                            last = nc.tensor.matmul(s[:, n, :], src[:, c, i * P:(i + 1) * P], fcT[:, c, 512 * n:512 * n + 512],
                                                    start=(m == 0), stop=(m == 2 * CC - 1))
                    last.then_inc(fc[0], 1)

                def sink_scores(o):
                    wait(pe, bd_ok, f)
                    nc.tensor.matmul(o[:, 0:H * SINK], idb[:], msink[:], start=True, stop=False, skip_group_check=True)
                    for i in range(TT_):
                        for t in range(NT):
                            last = nc.tensor.matmul(o[:, i * H * SINK:(i + 1) * H * SINK], Q[:, t, i * P:(i + 1) * P], BDH[:, t, 0:H * SINK],
                                                    start=False, stop=(t == NT - 1), skip_group_check=True)
                    return last

                def window_scores(r):
                    if r == 0:
                        if not back:
                            pe.wait_ge(ld_const, N_CONST)
                        wait(pe, q_ok, f)
                        wait(pe, kh_ok, f)
                    s = slot("f_p1", r)
                    q0, k0, heads, mask = (0, 0, range(NT), mask0) if r < 2 else (P, BLK, range(2 * (r % 2), 2 * (r % 2) + 2), mask1)
                    n, gp = mask.shape[1], (r if r < 2 else (r - 2) // 2)
                    for a in range(2):
                        nc.tensor.matmul(s[:, a, 0:n * len(heads)].rearrange("p (t k) -> p t k", t=len(heads)), idb[:],
                                         mask[:].unsqueeze(1).to_broadcast([P, len(heads), n]), start=True, stop=False, skip_group_check=True)
                    for j, t in enumerate(heads):
                        for a in range(2):
                            g = 32 * (2 * gp + a)
                            last = nc.tensor.matmul(s[:, a, n * j:n * j + n], Q[g:g + 32, t, q0:q0 + P], KH[g:g + 32, t, k0:k0 + n],
                                                    start=False, stop=True, skip_group_check=True)
                    if r == 5:
                        last = sink_scores(s[:, 0, 512 - TT_ * H * SINK:512])
                    last.then_inc(s1[0], 1)

                def transposed_rows():
                    s = slot("f_tr")
                    if not back:
                        pe.wait_ge(w_lo, N_LO)
                    wait(pe, xn_ok, f)
                    for c in range(CC):
                        for i in range(TT_):
                            nc.tensor.transpose(s[:, 0, c * T + i * P:c * T + (i + 1) * P], xn[:, i, c * P:(c + 1) * P], idf[:])
                    wait(pe, tx_ok, f)
                    for c in range(CC):
                        for i in range(TT_):
                            last = nc.tensor.transpose(s[:, 1, c * T + i * P:c * T + (i + 1) * P], txs[:, i, c * P:(c + 1) * P], idf[:])
                    last.then_inc(tr_x[0], 1)

                def latents():
                    wait(pe, xh_ok, f)
                    wait(pe, xl_ok, f)
                    if back:
                        wait(pe, exs, b)
                    for n, (x_half, w_half) in enumerate(HALVES):
                        for c in range(CC):
                            last = nc.tensor.matmul(aux[0:L, 0:T], wkvT[:, w_half, c, :], (xhT, xlT)[x_half][:, c, :],
                                                    start=(n == 0 and c == 0), stop=(n == 2 and c == CC - 1))
                    last.then_inc(mm_lat[0], 1)
                    if not back:
                        weight_totals()

                if back:
                    fc_tile(0)
                    wait(pe, m_ok, b)
                    wait_before(pe, xa_ok, b)
                    for i in range(TT_):
                        last = nc.tensor.transpose(aux[BLK:BLK + 2 * H, 0:T // 2].bitcast(bf16)[:, i * P:(i + 1) * P],
                                                   mhl[:, i].rearrange("p a h -> p (a h)"), idb[:])
                    last.then_inc(mT[0], 1)
                    fc_tile(1)
                    if front:
                        transposed_rows()
                    wait(pe, mT_ok, b); wait(pe, kl_ok, b)
                    nc.tensor.matmul(aux[:, 0:T], bias[:, 2 * H, :], mov[:], start=True, stop=False, skip_group_check=True)
                    for t in range(NT):
                        for K in (BDH, BDL):
                            last = nc.tensor.matmul(aux[:, 0:T], K[:, t, :], Q[:, t, :], start=False,
                                                    stop=(t == NT - 1 and K is BDL), skip_group_check=True)
                    last.then_inc(s2s[0], 1)
                    for r in range(4):
                        gp, tp = divmod(r, 2)
                        s = slot("p2", r)
                        for j in range(2):
                            for a in range(2):
                                hm = NT * (2 * gp + a) + 2 * tp + j
                                nc.tensor.matmul(s[:, a, T * j:T * j + BLK], bias[:, hm, :], mov[:, 0:BLK],
                                                 start=(j == 0), stop=False, skip_group_check=True)
                                nc.tensor.matmul(s[:, a, T * j + BLK:T * j + T], bias[:, H + hm, :], mov[:, BLK:T],
                                                 start=False, stop=False, skip_group_check=True)
                        for j in range(2):
                            t = 2 * tp + j
                            for q0, n, k0 in ((0, P, 0), (P, BLK, BLK), (P + BLK, BLK, P)):
                                for K in (KH, KL):
                                    for a in range(2):
                                        g = 32 * (2 * gp + a)
                                        last = nc.tensor.matmul(s[:, a, T * j + q0:T * j + q0 + n], K[g:g + 32, t, k0:k0 + P],
                                                                Q[g:g + 32, t, q0:q0 + n], start=False, stop=True, skip_group_check=True)
                        last.then_inc(s2[0], 1)
                        if front and r == 2:
                            latents()
                if front:
                    if not back:
                        transposed_rows()
                        latents()

                def q_products():
                    s = slot("f_q")
                    for t in range(NT):
                        for n, (x_half, w_half) in enumerate(HALVES):
                            for c in range(CC):
                                last = nc.tensor.matmul(s[:, t // 2, (t % 2) * T:(t % 2 + 1) * T],
                                                        wqT[:, w_half, c, G * t:G * t + G].rearrange("p h d e -> p (h d e)"), (xhT, xlT)[x_half][:, c, :],
                                                        start=(n == 0 and c == 0), stop=(n == 2 and c == CC - 1), skip_group_check=True)
                    last.then_inc(mm_q[0], 1)

                def k_products():
                    wait(pe, lath_ok, f)
                    wait(pe, latl_ok, f)
                    s = slot("f_k")
                    for t in range(NT):
                        for n, (l_half, w_half) in enumerate(HALVES):
                            last = nc.tensor.matmul(s[:, t // 2, (t % 2) * T:(t % 2 + 1) * T],
                                                    wkT[:, w_half, G * t:G * t + G].rearrange("p h d e -> p (h d e)"), (latH, latL)[l_half][:],
                                                    start=(n == 0), stop=(n == 2), skip_group_check=True)
                    last.then_inc(mm_k[0], 1)

                def hidden_transposed(i):
                    wait(pe, t2, b, i + 1)
                    s = slot("t2T", i)
                    for k in range(FC):
                        last = nc.tensor.transpose(s[:, k // 4, (k % 4) * P:(k % 4 + 1) * P], t2s[:, i, k * P:(k + 1) * P], idf[:])
                    last.then_inc(tr_h[0], 1)

                def values(probs, probs_sink, parts_v, first):
                    for i, o in ((0, acc), (1, aux)):
                        for n, (_, vsink) in enumerate(parts_v):
                            nc.tensor.matmul(o[:, 0:H * VW], probs_sink[:, i * P:(i + 1) * P], vsink[:].rearrange("p h d -> p (h d)"),
                                             start=(first and n == 0), stop=False, skip_group_check=True)
                        for h in range(H):
                            t, g = divmod(h, G)
                            parts = ((0, P, 0, 0),) if i == 0 else ((0, BLK, P, 1), (BLK, BLK, P + BLK, 2))
                            for p0, m, q0, v in parts:
                                for w, _ in parts_v:
                                    last = nc.tensor.matmul(o[p0:p0 + m, h * VW:(h + 1) * VW], probs[:, g, t, q0:q0 + m], w[:, v, h, :],
                                                            start=False, stop=not first, skip_group_check=True)
                        if not first:
                            last.then_inc(pv[0], 1)

                if front:
                    q_products()
                    k_products()
                if back:
                    hidden_transposed(0)
                    wait(pe, exs, b)
                    wait(pe, exh, b)
                    wait_before(pe, o_ok, b)
                    if front:
                        wait(pe, latl_ok, f)
                    values(EH, ESH, ((VH, VSH), (VL, VSL)), True)
                    hidden_transposed(1)
                    wait(pe, els, b)
                    wait(pe, el_ok, b)
                    values(EL, ESL, ((VH, VSH),), False)
                if front:
                    s = slot("f_v")
                    for j in range(3):
                        for n, (l_half, w_half) in enumerate(HALVES):
                            last = nc.tensor.matmul(s[:, j // 2, (j % 2) * C:(j % 2 + 1) * C], (latH, latL)[l_half][:, BLK * j:BLK * j + P],
                                                    wvT[:, w_half], start=(n == 0), stop=(n == 2), skip_group_check=True)
                    for n, (l_half, w_half) in enumerate(HALVES):
                        last = nc.tensor.matmul(s[0:H * SINK, 1, C:2 * C], (latSH, latSL)[l_half][:].rearrange("p h s -> p (h s)"), wvT[:, w_half],
                                                start=(n == 0), stop=(n == 2), skip_group_check=True)
                    last.then_inc(mm_v[0], 1)
                if back:
                    wait(pe, y_ok, b)
                    for c in range(CC):
                        for i in range(TT_):
                            last = nc.tensor.transpose(aux[:, c * T + i * P:c * T + (i + 1) * P], y[:, i, c * P:(c + 1) * P], idf[:])
                    last.then_inc(tr_y[0], 1)
                for i in range(TT_):
                    if back:
                        wait(pe, t2h_ok, b, i + 1)
                        wait(pe, t2l_ok, b, i + 1)
                        for k in range(FC):
                            for src in (t2h, t2l):
                                last = nc.tensor.matmul(acc[:, i * C:(i + 1) * C], src[:, i, k, :], prT[:, k, :],
                                                        start=(k == 0 and src is t2h), stop=(k == FC - 1 and src is t2l), skip_group_check=True)
                        last.then_inc(pr[0], 1)
                    if i == 1 and back:
                        wait(pe, yh_ok, b)
                        wait(pe, yl_ok, b)
                        for j in range(TT_):
                            for n, (y_half, w_half) in enumerate(HALVES):
                                for c in range(CC):
                                    last = nc.tensor.matmul(aux[:, j * C:(j + 1) * C], (yhT, ylT)[y_half][:, c, j * P:(j + 1) * P], woT[:, w_half, c, :],
                                                            start=(n == 0 and c == 0), stop=(n == 2 and c == CC - 1), skip_group_check=True)
                        last.then_inc(mm_wo[0], 1)
                    if front:
                        for r in range(3 * i, 3 * i + 3):
                            window_scores(r)
                if front and not back:
                    weights()

            schedule(pe, body)


def shape_constants():
    import numpy as np

    def bf16_bits(a):
        return (np.ascontiguousarray(a, np.float32).view(np.uint32) >> 16).astype(np.uint16)

    k = {}
    k["c_idf"] = np.eye(P, dtype=np.float32)
    k["c_idh"] = np.eye(P, dtype=np.float16)
    k["c_idb"] = bf16_bits(np.eye(P))
    q, j = np.arange(T)[:, None], np.arange(T)[None, :]
    band = (j <= q) & (j >= q - (WINDOW - 1))
    mask = np.where(band, 0.0, MASKED)
    k["c_mask0"] = bf16_bits(mask[0:P, 0:P])
    k["c_mask1"] = bf16_bits(mask[P:T, BLK:T])
    sink = np.where(np.arange(SINK)[None, :] <= q - WINDOW, 0.0, MASKED)
    k["c_msink"] = bf16_bits(np.tile(sink[0:P], (1, H)))
    bias = np.zeros((BIAS_ROWS, 2 * H + 1, P), np.float32)
    for hm in range(H):
        bias[0:BLK, hm] = mask[0:BLK, 0:P]
        bias[0:BLK, H + hm] = mask[BLK:P, 0:P]
        for n in (hm, H + hm):
            bias[BLK + hm, n] = bias[BLK + H + hm, n] = 1.0
        bias[BLK + hm, 2 * H, hm * SINK:(hm + 1) * SINK] = 1.0
        bias[BLK + H + hm, 2 * H, hm * SINK:(hm + 1) * SINK] = 1.0
        for s in range(SINK):
            bias[BLK + 2 * H + s, 2 * H, hm * SINK + s] = MASKED
    k["c_bias"] = bf16_bits(bias)
    mov = np.zeros((BIAS_ROWS, T), np.float32)
    mov[0:BLK] = np.tile(np.eye(BLK), (1, T // BLK))
    mov[BLK + 2 * H:] = (sink != 0).T
    k["c_mov"] = bf16_bits(mov)
    p = np.arange(P)
    k["c_rowlo"] = -((p % 32) >= HD).astype(np.float32)[:, None]
    k["c_gmask"] = (p[:, None] // 32 == np.arange(G)[None, :]).astype(np.float32)
    hm = np.arange(H * SINK) // SINK
    own = ((hm % NT) * G + hm // NT)[:, None] == np.arange(H)[None, :]
    k["c_vsmask"] = own.astype(np.float32)
    k["c_vsones"] = np.zeros((H * SINK, H, VW), np.float16)
    k["c_vsones"][:, :, HD] = own
    return k


_INS = ["L0_attn_x", "L0_attn_Wq", "L0_attn_Wkv_down", "L0_attn_Wk_up", "L0_attn_Wv_up", "L0_attn_Wo",
        "L0_ffn_w_fc", "L0_ffn_w_proj"]


def kernel(**inputs):
    import numpy as np
    import concourse.bacc as bacc
    from concourse.bass_utils import run_bass_kernel_spmd

    nc = bacc.Bacc("TRN2", target_bir_lowering=False, num_devices=1)
    arrays, args = {}, []
    given = {name: np.ascontiguousarray(inputs[name]) for name in _INS}
    for name, a in {**given, **shape_constants()}.items():
        arrays[f"in_{name}"] = a
        args.append(nc.dram_tensor(f"in_{name}", a.shape, mybir.dt.from_np(a.dtype), kind="ExternalInput").ap())
    args.append(nc.dram_tensor("out_0", (B, T, C), mybir.dt.float32, kind="ExternalOutput").ap())
    layer_kernel(nc, *args)
    r = run_bass_kernel_spmd(nc, [arrays], core_ids=[0])
    return r.results[0]["out_0"]
```

```python
import concourse.bass as bass
from concourse import mybir
from contextlib import ExitStack

B, T, C, L, H, F = 4, 256, 256, 64, 16, 1024
HD = C // H
P = 128
WINDOW, SINK = 64, 4
TT_ = T // P
CC = C // P
FC = F // P
G = 4
NT = H // G
BLK = 64
VW = HD + 1
QB = 128.0
LN_EPS, FFN_EPS = 1e-5, 1e-6
BIAS_ROWS = BLK + 2 * H + SINK
MASKED = -(2.0 ** 100)
NORM = 2.0 ** 8
KV_SCALE = 2.0 ** -6
LEAST = 2.0 ** -32


def layer_kernel(nc, x, wq, wkv, wku, wvu, wo, wfc, wproj, c_idf, c_idh, c_idb, c_mask0, c_mask1,
                 c_msink, c_bias, c_mov, c_rowlo, c_gmask, c_vsmask, c_vsones, out):
    fp32 = mybir.dt.float32
    bf16, fp16 = mybir.dt.bfloat16, mybir.dt.float16
    ALU = mybir.AluOpType
    ACT = mybir.ActivationFunctionType
    AX = mybir.AxisListType

    ctx = ExitStack()
    with ctx:
        def sb(name, shape, dt):
            return ctx.enter_context(nc.sbuf_tensor(name, shape, dt))

        def sem(name):
            return ctx.enter_context(nc.semaphore(name))

        idf = sb("idf", [P, P], fp32)
        idh = sb("idh", [P, P], fp16)
        idb = sb("idb", [P, P], bf16)
        mask0 = sb("mask0", [P, P], bf16)
        mask1 = sb("mask1", [P, T - BLK], bf16)
        msink = sb("msink", [P, H * SINK], bf16)
        bias = sb("bias", [BIAS_ROWS, 2 * H + 1, P], bf16)
        mov = sb("mov", [BIAS_ROWS, T], bf16)
        rowlo = sb("rowlo", [P, 1], fp32)
        gmask = sb("gmask", [P, G], fp32)
        vsmask = sb("vsmask", [H * SINK, H], fp32)
        ones = sb("ones", [P, P], fp32)
        neghalf = sb("neghalf", [P, 5], fp32)
        wq_r = sb("wq_r", [P, CC, C], fp32)
        wkv_r = sb("wkv_r", [L, C], fp32)
        wku_r = sb("wku_r", [P, CC, 2, L], fp32)
        wvu_r = sb("wvu_r", [P, CC, 2, L], fp32)
        wo_r = sb("wo_r", [P, CC, C], fp32)
        wfc_r = sb("wfc_r", [P, FC, C], fp32)
        wpr_r = sb("wpr_r", [P, CC, F], fp32)
        wqT = sb("wqT", [P, 2, CC, H, 2, HD], fp16)
        wkvT = sb("wkvT", [P, 2, CC, 2, L], fp16)
        wkT = sb("wkT", [P, 2, H, 2, HD], fp16)
        wvT = sb("wvT", [P, 2, C], fp16)
        woT = sb("woT", [P, 2, CC, C], fp16)
        neg_t = sb("neg_t", [P, 2, FC * C], fp16)
        tern = sb("tern", [P, 2, FC * C], fp16)
        fcT = sb("fcT", [P, CC, F], fp16)
        prT = sb("prT", [P, FC, C], fp16)
        wsum = sb("wsum", [P, 2, FC], fp32)
        gam = sb("gam", [P, 2], fp32)
        thr = sb("thr", [P, 2], fp32)
        nthr = sb("nthr", [P, 2], fp32)
        gam128 = sb("gam128", [P, 2], fp32)
        wsq = sb("wsq", [P, 5, 2], fp32)
        junk = sb("junk", [P, 5, CC * C], bf16)
        sq = sb("sq", [P, 5], fp32)
        rsq = sb("rsq", [P, 5], fp32)
        root = sb("root", [P, 5], fp32)
        sc = sb("sc", [P, 5], fp32)
        rr = sb("rr", [P, 2], fp32)
        un = sb("un", [P, 2], fp32)
        xin = sb("xin", [P, TT_, C], fp32)
        st1 = sb("st1", [P, TT_, 6], fp32)
        mv1 = sb("mv1", [P, TT_, 2], fp32)
        ve1 = sb("ve1", [P, TT_], fp32)
        rs1 = sb("rs1", [P, TT_], fp32)
        xn = sb("xn", [P, TT_, C], fp32)
        st2 = sb("st2", [P, TT_, 6], fp32)
        mv2 = sb("mv2", [P, TT_, 2], fp32)
        ve2 = sb("ve2", [P, TT_], fp32)
        rs2 = sb("rs2", [P, TT_], fp32)
        cx = sb("cx", [P, TT_, C], fp32)
        nmx = sb("nmx", [P, TT_], fp32)
        gx = sb("gx", [P, TT_], fp32)
        gxq = sb("gxq", [P, TT_], fp32)
        gxr = sb("gxr", [P, TT_], fp32)
        ga1 = sb("ga1", [P, TT_], fp32)
        a1 = sb("a1", [P, TT_], fp32)
        txs = sb("txs", [P, TT_, C], fp32)
        xhT = sb("xhT", [P, CC, T], fp16)
        xlT = sb("xlT", [P, CC, T], fp16)
        thT = sb("thT", [P, CC, T], fp16)
        tlT = sb("tlT", [P, CC, T], fp16)
        lat = sb("lat", [P, T], fp16)
        latS = sb("latS", [P, H, SINK], fp16)
        qh = sb("qh", [P, NT * T], fp16)
        Q = sb("Q", [P, NT, T], fp16)
        KH = sb("KH", [P, NT, T], fp16)
        KL = sb("KL", [P, NT, T], fp16)
        BDH = sb("BDH", [P, NT, P], fp16)
        BDL = sb("BDL", [P, NT, P], fp16)
        VH = sb("VH", [P, 3, H, VW], fp16)
        VL = sb("VL", [P, 3, H, VW], fp16)
        vs32 = sb("vs32", [H * SINK, H, HD], fp32)
        VSH = sb("VSH", [H * SINK, H, VW], fp16)
        VSL = sb("VSL", [H * SINK, H, VW], fp16)
        mx = sb("mx", [P, TT_, H], fp32)
        smx = sb("smx", [P, TT_, H], fp32)
        mm = sb("mm", [P, TT_, H], fp32)
        mhl = sb("mhl", [P, TT_, 2, H], bf16)
        E32 = sb("E32", [P, 4, 2, 2 * T], fp32)
        EH = sb("EH", [P, G, NT, T], fp16)
        EL = sb("EL", [P, G, NT, T], fp16)
        ES32 = sb("ES32", [H * SINK, T], fp32)
        ESH = sb("ESH", [H * SINK, T], fp16)
        ESL = sb("ESL", [H * SINK, T], fp16)
        rden = sb("rden", [P, TT_, H], fp32)
        y = sb("y", [P, TT_, C], fp32)
        yhT = sb("yhT", [P, CC, T], fp16)
        ylT = sb("ylT", [P, CC, T], fp16)
        xres = sb("xres", [P, TT_, C], fp32)
        att = sb("att", [P, TT_, C], fp32)
        ffn = sb("ffn", [P, TT_, C], fp32)
        xff = sb("xff", [P, TT_, C], fp32)
        ob = sb("ob", [P, TT_, C], fp32)
        gl = sb("gl", [P, TT_, F], fp32)
        sth = sb("sth", [P, TT_, 2, 6], fp32)
        mvh = sb("mvh", [P, TT_, 2], fp32)
        veh = sb("veh", [P, TT_], fp32)
        rsh = sb("rsh", [P, TT_], fp32)
        ch = sb("ch", [P, TT_, F], fp32)
        t2s = sb("t2s", [P, TT_, F], fp32)
        gh = sb("gh", [P, TT_], fp32)
        ghr = sb("ghr", [P, TT_], fp32)
        ga2 = sb("ga2", [P, TT_], fp32)
        a2 = sb("a2", [P, TT_], fp32)
        t2h = sb("t2h", [P, TT_, FC, P], fp16)
        t2l = sb("t2l", [P, TT_, FC, P], fp16)

        ring = [ctx.enter_context(nc.psum_tensor(f"ring{i}", [P, 2, 512], fp32)) for i in range(3)]
        aux = ctx.enter_context(nc.psum_tensor("aux", [P, 512], fp32))
        acc = ctx.enter_context(nc.psum_tensor("acc", [P, 512], fp32))

        ps_wq, ps_wku, ps_wvu = ring[0][:, 0, :], ring[0][:, 1, 0:C], ring[0][:, 1, C:2 * C]
        ps_wkv, ps_wo = ring[1][:, 0, 0:CC * L], ring[1][:, 1, :]

        def stage(name, per):
            return sem(name), per, 0

        primed = []

        def primed_stage(name, per):
            primed.append(sem(name))
            return primed[-1], per, 1

        ld_id = sem("ld_id"); ld_const = sem("ld_const"); ld_wf = sem("ld_wf"); ld_wp = sem("ld_wp")
        ld_w = [sem(f"ld_w{n}") for n in ("q", "kv", "ku", "vu", "o")]
        ld_x = stage("ld_x", 16); ld_res = stage("ld_res", 16); st_out = primed_stage("st_out", 16)
        memsets = sem("memsets")
        N_SET = 8
        N_CONST = 16 * 11
        passed = sem("passed")
        w_tr = sem("w_tr"); w_ev = sem("w_ev"); w_lo = sem("w_lo"); w_sq = sem("w_sq"); w_sqtot = sem("w_sqtot")
        bounds = sem("bounds"); roots = sem("roots"); scales = sem("scales"); undo = sem("undo")
        w_abs = sem("w_abs"); w_tot = sem("w_tot"); means = sem("means"); w_thr = sem("w_thr"); w_neg = sem("w_neg"); w_tern = sem("w_tern")
        dve_pro = sem("dve_pro"); pool_pro = sem("pool_pro")
        tr_x = stage("tr_x", 1); mm_lat = stage("mm_lat", 1); mm_q = stage("mm_q", 1)
        mm_k = stage("mm_k", 1); mm_v = stage("mm_v", 1)
        xh_ok = stage("xh_ok", 1); xl_ok = stage("xl_ok", 1); th_ok = stage("th_ok", 1); tl_ok = stage("tl_ok", 1)
        lath_ok = stage("lath_ok", 2); latl_ok = stage("latl_ok", 2); qh_ok = stage("qh_ok", 1); q_ok = stage("q_ok", 1)
        kh_ok = stage("kh_ok", 1); kl_ok = stage("kl_ok", 1); bd_ok = stage("bd_ok", 2)
        vh_ok = stage("vh_ok", 1); v_ok = stage("v_ok", 1); vs_ok = stage("vs_ok", 3)
        var1 = stage("var1", TT_); rstd1 = stage("rstd1", 1); xn_ok = stage("xn_ok", TT_)
        nmx_ok = stage("nmx_ok", 1); cx_ok = stage("cx_ok", TT_); gx_ok = stage("gx_ok", TT_); gxq_ok = stage("gxq_ok", 1); tx_ok = stage("tx_ok", TT_); a1_ok = stage("a1_ok", 1)
        pool_f = stage("pool_f", 4)
        s1 = stage("s1", 6); red1 = stage("red1", 6); red1s = stage("red1s", 1)
        mm_ok = stage("mm_ok", 1); m_ok = stage("m_ok", 2); mT = stage("mT", 1); mT_ok = stage("mT_ok", 1)
        s2 = stage("s2", 4); s2s = primed_stage("s2s", 1); ex = primed_stage("ex", 4); exh = stage("exh", 4); el_ok = primed_stage("el_ok", 4); exs = stage("exs", 2); els = stage("els", 1)
        pv = primed_stage("pv", TT_); y_ok = stage("y_ok", TT_); tr_y = primed_stage("tr_y", 1)
        yh_ok = stage("yh_ok", 1); yl_ok = stage("yl_ok", 1); mm_wo = primed_stage("mm_wo", 1)
        fc = stage("fc", TT_); gelu = primed_stage("gelu", TT_); ch_ok = stage("ch_ok", TT_); t2 = primed_stage("t2", TT_); gh_ok = stage("gh_ok", TT_)
        tr_h = stage("tr_h", TT_); t2h_ok = stage("t2h_ok", TT_); t2l_ok = primed_stage("t2l_ok", TT_)
        pr = primed_stage("pr", TT_); a2_ok = primed_stage("a2_ok", TT_); pool_b = stage("pool_b", 6)
        att_ok = primed_stage("att_ok", 1); ffn_ok = primed_stage("ffn_ok", TT_); xa_ok = primed_stage("xa_ok", 1); o_ok = primed_stage("o_ok", 1)
        DF, DB = 7, 10
        dve_f = stage("dve_f", DF); dve_b = stage("dve_b", DB)

        def wait(eng, st, b, k=None):
            s, per, start = st
            v = b * per + (per if k is None else k) + start
            if not isinstance(v, int) or v > start:
                eng.wait_ge(s, v)

        def wait_before(eng, st, b):
            wait(eng, st, b, 0)

        def wait_apart(eng, st, b, k=None):
            wait(eng, st, b, k)
            if not isinstance(b, int):
                eng.sem_inc(passed, 1)

        x_v = x.rearrange("b (i p) c -> b p i c", p=P)
        out_v = out.rearrange("b (i p) c -> b p i c", p=P)

        USES = (
            [("fc", i, [(gelu, i + 1)]) for i in range(TT_)]
            + [("f_tr", 0, [(xl_ok, 1), (tl_ok, 1)])]
            + [("p2", r, [(exh, r + 1)]) for r in range(4)]
            + [("f_q", 0, [(q_ok, 1)]), ("f_k", 0, [(kl_ok, 1)])]
            + [("t2T", i, [(t2l_ok, i + 1)]) for i in range(TT_)]
            + [("f_v", 0, [(v_ok, 1), (vs_ok, 1)])]
            + [("f_p1", r, [(red1, r + 1)] + ([(red1s, 1)] if r == 5 else [])) for r in range(6)]
        )
        NU = len(USES)
        assert NU % 3 == 0
        AT = {(n, i): u for u, (n, i, _) in enumerate(USES)}

        def take(eng, name, i, b, back, front):
            u = AT[(name, i)]
            v, cur = u, True
            while True:
                v -= 3
                if v < 0:
                    v += NU
                    if not cur:
                        break
                    cur = False
                is_front = USES[v][0].startswith("f_")
                if cur and not (front if is_front else back):
                    continue
                if not cur and not is_front and not back:
                    continue
                if not cur and is_front and not back:
                    break
                for st, k in USES[v][2]:
                    if cur:
                        wait(eng, st, b + 1 if is_front else b, k)
                    elif is_front:
                        wait(eng, st, b, k)
                    else:
                        wait_before(eng, st, b)
                break
            return ring[u % 3]

        def hidden_slot(i, front):
            return ring[AT[("t2T", i)] % 3] if front else ring[AT[("p2", 1 + i)] % 3]

        def ffn_bank(front):
            return acc if front else ring[AT[("p2", 3)] % 3][:, 0, :]

        def schedule(eng, body):
            body(-2, False, False, True)
            body(-1, False, True, True)
            with eng.Fori(0, B - 2) as b:
                body(b, True, True, True)
            body(B - 2, True, True, False)
            body(B - 1, True, False, False)

        block = ctx.enter_context(nc.Block())

        @block.sync
        def _(sp):
            sp.dma_start(idf[:], c_idf).then_inc(ld_id, 16)
            sp.dma_start(xin[:], x_v[0]).then_inc(ld_x[0], 16)
            for d in range(2):
                sp.dma_start(wku_r[:, :, d, :], wku.rearrange("(c p) k -> p c k", p=P)).then_inc(ld_w[2], 16)
            sp.dma_start(wo_r[:], wo.rearrange("(c p) k -> p c k", p=P)).then_inc(ld_w[4], 16)
            sp.dma_start(wfc_r[:], wfc.rearrange("(c p) k -> p c k", p=P)).then_inc(ld_wf, 16)
            sp.dma_start(wpr_r[:], wproj.rearrange("(c p) k -> p c k", p=P)).then_inc(ld_wp, 16)
            for dst, src in ((rowlo, c_rowlo), (gmask, c_gmask), (vsmask, c_vsmask), (idh, c_idh), (VSH, c_vsones),
                             (idb, c_idb), (mask0, c_mask0), (mask1, c_mask1), (msink, c_msink), (mov, c_mov),
                             (bias, c_bias)):
                view = dst[:].bitcast(mybir.dt.uint16) if dst.dtype == bf16 else dst[:]
                sp.dma_start(view, src).then_inc(ld_const, 16)

            def body(b, back, front, rows):
                if back:
                    wait_before(sp, xa_ok, b)
                    sp.dma_start(xres[:], x_v[b]).then_inc(ld_res[0], 16)
                    wait(sp, o_ok, b)
                    sp.dma_start(out_v[b], ob[:]).then_inc(st_out[0], 16)

            schedule(sp, body)
            wait(sp, st_out, B - 1)

        @block.gpsimd
        def _(pool):
            for n, (dst, v) in enumerate(((neghalf, -0.5), (wsq, 0.0), (ones, 1.0), (BDH, 0.0), (BDL, 0.0),
                                          (VH, 1.0), (VL, 0.0), (VSL, 0.0))):
                nc.gpsimd.memset(dst[:], v).then_inc(memsets, 1)
            pool.wait_ge(memsets, N_SET)
            for s in primed:
                pool.sem_inc(s, 1)

            def norms():
                pool.wait_ge(bounds, 1)
                nc.gpsimd.tensor_tensor(rsq[:], sq[:], neghalf[:], ALU.pow).then_inc(pool_pro, 1)
                pool.wait_ge(pool_pro, 1)
                nc.gpsimd.tensor_tensor(root[:], sq[:], rsq[:], ALU.mult).then_inc(roots, 1)

            def low_half(b, r):
                gp, tp = divmod(r, 2)
                wait(pool, ex, b, r + 1)
                wait(pool, exh, b, r + 1)
                if r == 0:
                    wait_before(pool, pv, b)
                at = (slice(None), slice(2 * gp, 2 * gp + 2), slice(2 * tp, 2 * tp + 2))
                nc.gpsimd.tensor_tensor(EL[at].rearrange("p g t q -> p g (t q)"), E32[:, r],
                                        EH[at].rearrange("p g t q -> p g (t q)"), ALU.subtract).then_inc(el_ok[0], 1)

            def body(b, back, front, rows):
                f = b + 1
                n = b + 2
                if back:
                    low_half(b, 0)
                if rows:
                    wait_apart(pool, var1, n)
                    nc.gpsimd.tensor_scalar(ve1[:], mv1[:, :, 1], LN_EPS, None, ALU.add).then_inc(pool_f[0], 1)
                    wait(pool, pool_f, n, 1)
                    nc.gpsimd.tensor_tensor(rs1[:], ve1[:], neghalf[:, 0:TT_], ALU.pow).then_inc(rstd1[0], 1)
                if back:
                    for r in range(1, 4):
                        low_half(b, r)
                    wait(pool, exs, b)
                    nc.gpsimd.tensor_tensor(ESL[:], ES32[:], ESH[:], ALU.subtract).then_inc(els[0], 1)
                if front:
                    if back:
                        wait(pool, gelu, b)
                    else:
                        pool.wait_ge(means, 1)
                    wait_apart(pool, pool_f, b + 1, 4)
                    nc.gpsimd.tensor_scalar(a1[:], ga1[:], gam128[:, 0:1], None, ALU.mult).then_inc(a1_ok[0], 1)
                    if not back:
                        pool.wait_ge(w_thr, 2)
                        nc.gpsimd.tensor_scalar(neg_t[:, 1], wpr_r[:].rearrange("p a k -> p (a k)"), nthr[:, 1:2], None, ALU.is_lt).then_inc(w_neg, 1)
                if back:
                    for i in range(TT_):
                        wait_apart(pool, gh_ok, b, i + 1)
                        nc.gpsimd.tensor_scalar(veh[:, i:i + 1], mvh[:, i, 1:2], FFN_EPS, None, ALU.add).then_inc(pool_b[0], 1)
                        wait(pool, pool_b, b, 3 * i + 1)
                        nc.gpsimd.tensor_tensor(rsh[:, i:i + 1], veh[:, i:i + 1], neghalf[:, 0:1], ALU.pow).then_inc(pool_b[0], 1)
                        wait(pool, pool_b, b, 3 * i + 2)
                        nc.gpsimd.tensor_tensor(ga2[:, i:i + 1], rsh[:, i:i + 1], gh[:, i:i + 1], ALU.mult).then_inc(pool_b[0], 1)
                        if i == 0:
                            wait_before(pool, ffn_ok, b)
                        wait_apart(pool, pool_b, b, 3 * i + 3)
                        nc.gpsimd.tensor_scalar(a2[:, i:i + 1], ga2[:, i:i + 1], gam128[:, 1:2], None, ALU.mult).then_inc(a2_ok[0], 1)
                if rows:
                    if not (back or front):
                        norms()
                    wait_apart(pool, gx_ok, n)
                    nc.gpsimd.tensor_scalar(ve2[:], mv2[:, :, 1], FFN_EPS, None, ALU.add).then_inc(pool_f[0], 1)
                    wait(pool, pool_f, n, 2)
                    nc.gpsimd.tensor_tensor(rs2[:], ve2[:], neghalf[:, 0:TT_], ALU.pow).then_inc(pool_f[0], 1)
                    wait(pool, pool_f, n, 3)
                    if front:
                        wait(pool, a1_ok, n - 1)
                    nc.gpsimd.tensor_tensor(ga1[:], rs2[:], gx[:], ALU.mult).then_inc(pool_f[0], 1)
                if front:
                    if back:
                        wait(pool, pv, b)
                    wait_apart(pool, vs_ok, f, 1)
                    nc.gpsimd.tensor_copy(VSH[:, :, 0:HD], vs32[:]).then_inc(vs_ok[0], 1)
                    wait(pool, vs_ok, f, 2)
                    nc.gpsimd.tensor_tensor(VSL[:, :, 0:HD], vs32[:], VSH[:, :, 0:HD], ALU.subtract).then_inc(vs_ok[0], 1)
                if back:
                    wait(pool, ffn_ok, b)
                    wait(pool, ld_res, b)
                    nc.gpsimd.tensor_tensor(xff[:], ffn[:], xres[:], ALU.add).then_inc(xa_ok[0], 1)
                if back and front:
                    wait(pool, xa_ok, b)
                    wait(pool, att_ok, b)
                    wait_before(pool, st_out, b)
                    nc.gpsimd.tensor_tensor(ob[:], att[:], xff[:], ALU.add).then_inc(o_ok[0], 1)

            schedule(pool, body)

        @block.scalar
        def _(act):
            act.dma_start(wq_r[:], wq.rearrange("(c p) k -> p c k", p=P)).then_inc(ld_w[0], 16)
            act.dma_start(wkv_r[:], wkv).then_inc(ld_w[1], 16)
            for d in range(2):
                act.dma_start(wvu_r[:, :, d, :], wvu.rearrange("(c p) k -> p c k", p=P)).then_inc(ld_w[3], 16)

            for n, w in enumerate((wq_r, wkv_r, wku_r, wvu_r, wo_r)):
                act.wait_ge(ld_w[n], 32 if n in (2, 3) else 16)
                if n == 0:
                    act.wait_ge(memsets, N_SET)
                once = w[:, :, 0, :] if len(w.shape) == 4 else w[:] if len(w.shape) == 3 else w[:].unsqueeze(1)
                rows, a, k = once.shape
                nc.scalar.activation(junk[0:rows, n, 0:a * k].rearrange("p (a k) -> p a k", a=a), once, ACT.Square, accum_out=wsq[0:rows, n, 0:1]).then_inc(w_sq, 1)

            wait(act, xn_ok, 0)
            act.dma_start(xin[:], x_v[1]).then_inc(ld_x[0], 16)

            act.wait_ge(scales, 1)
            act.wait_ge(w_tr, 2)
            nc.scalar.activation(wkvT[:, 0], ps_wkv.rearrange("p (c l) -> p c l", c=CC).unsqueeze(2).to_broadcast([P, CC, 2, L]), ACT.Copy, scale=sc[:, 1:2]).then_inc(w_ev, 1)
            for c in range(CC):
                nc.scalar.activation(wqT[:, 0, c, :, :, :], ps_wq[:, c * C:(c + 1) * C].rearrange("p (h e) -> p h e", h=H).unsqueeze(2).to_broadcast([P, H, 2, HD]),
                                     ACT.Copy, scale=sc[:, 0:1]).then_inc(w_ev, 1)
            act.wait_ge(w_tr, 3)
            nc.scalar.activation(woT[:, 0], ps_wo.rearrange("p (c k) -> p c k", c=CC), ACT.Copy, scale=sc[:, 4:5]).then_inc(w_ev, 1)

            def up_weights():
                nc.scalar.activation(wkT[:, 0], ps_wku.rearrange("p (h e) -> p h e", h=H).unsqueeze(2).to_broadcast([P, H, 2, HD]),
                                     ACT.Copy, scale=sc[:, 2:3]).then_inc(w_ev, 1)
                nc.scalar.activation(wvT[:, 0], ps_wvu, ACT.Copy, scale=sc[:, 3:4]).then_inc(w_ev, 1)

            def body(b, back, front, rows):
                f = b + 1
                def exponentials(r):
                    gp, tp = divmod(r, 2)
                    at = (slice(None), slice(2 * gp, 2 * gp + 2), slice(2 * tp, 2 * tp + 2))
                    src = ring[AT[("p2", r)] % 3]
                    wait(act, s2, b, r + 1)
                    if r == 0:
                        wait_before(act, el_ok, b)
                    nc.scalar.activation(E32[:, r], src[:], ACT.Exp, scale=un[:, 0:1]).then_inc(ex[0], 1)
                    nc.scalar.activation(EH[at].rearrange("p g t q -> p g (t q)"), src[:], ACT.Exp, scale=un[:, 0:1]).then_inc(exh[0], 1)

                if back and rows:
                    wait(act, xn_ok, b + 1)
                    act.dma_start(xin[:], x_v[b + 2]).then_inc(ld_x[0], 16)
                if back:
                    for i in range(TT_):
                        wait(act, fc, b, i + 1)
                        if i == 0:
                            wait(act, a1_ok, b)
                            wait_before(act, t2, b)
                        nc.scalar.activation(gl[:, i, :], ring[AT[("fc", i)] % 3][:].rearrange("p a n -> p (a n)"),
                                             ACT.Gelu, scale=a1[:, i:i + 1]).then_inc(gelu[0], 1)
                if front:
                    wait(act, tr_x, f)
                    src = ring[AT[("f_tr", 0)] % 3]
                    if back:
                        wait(act, mm_q, b)
                    nc.scalar.activation(xhT[:], src[:, 0, :].rearrange("p (c t) -> p c t", c=CC), ACT.Copy).then_inc(xh_ok[0], 1)
                    if back:
                        wait(act, fc, b)
                    nc.scalar.activation(thT[:], src[:, 1, :].rearrange("p (c t) -> p c t", c=CC), ACT.Copy).then_inc(th_ok[0], 1)
                    if not back:
                        up_weights()
                if back:
                    wait(act, s2s, b)
                    wait_before(act, pv, b)
                    for e in (ES32, ESH):
                        nc.scalar.activation(e[:], aux[0:H * SINK, 0:T], ACT.Exp, scale=un[0:H * SINK, 0:1]).then_inc(exs[0], 1)
                    for r in range(3):
                        exponentials(r)
                if front:
                    wait(act, mm_lat, f)
                    if back:
                        wait(act, mm_v, b)
                    nc.scalar.activation(lat[:], aux[:, 0:T], ACT.Copy).then_inc(lath_ok[0], 1)
                    nc.scalar.activation(latS[:], aux[:, 0:SINK].unsqueeze(1).to_broadcast([P, H, SINK]),
                                         ACT.Copy).then_inc(lath_ok[0], 1)
                    if not back:
                        weights()
                if back:
                    exponentials(3)
                if front:
                    wait(act, mm_q, f)
                    if back:
                        wait(act, q_ok, b)
                    nc.scalar.activation(qh[:], ring[AT[("f_q", 0)] % 3][:].rearrange("p a n -> p (a n)"), ACT.Copy).then_inc(qh_ok[0], 1)
                    wait(act, mm_k, f)
                    if back:
                        wait(act, s2s, b)
                    nc.scalar.activation(KH[:].rearrange("p t n -> p (t n)"), ring[AT[("f_k", 0)] % 3][:].rearrange("p a n -> p (a n)"),
                                         ACT.Copy, scale=KV_SCALE).then_inc(kh_ok[0], 1)
                def hidden_high(i):
                    wait(act, tr_h, b, i + 1)
                    if i == 0:
                        wait_before(act, pr, b)
                    nc.scalar.activation(t2h[:, i].rearrange("p k n -> p (k n)"), hidden_slot(i, front)[:].rearrange("p a n -> p (a n)"),
                                         ACT.Copy).then_inc(t2h_ok[0], 1)

                if back:
                    hidden_high(0)
                if back and rows:
                    wait(act, nmx_ok, b + 2)
                    for i in range(TT_):
                        nc.scalar.activation(cx[:, i, :], xn[:, i, :], ACT.Identity, bias=nmx[:, i:i + 1]).then_inc(cx_ok[0], 1)
                if back:
                    hidden_high(1)
                if front:
                    wait(act, mm_v, f)
                    if back:
                        wait(act, pv, b)
                    else:
                        act.wait_ge(memsets, N_SET)
                    slot = ring[AT[("f_v", 0)] % 3]
                    nc.scalar.activation(VH[:, :, :, 0:HD], slot[:].rearrange("p a n -> p (a n)")[:, 0:3 * C]
                                         .rearrange("p (j h d) -> p j h d", j=3, h=H), ACT.Copy, scale=KV_SCALE).then_inc(vh_ok[0], 1)
                    if not back:
                        weights_transposed()
                def transposed_high():
                    wait(act, tr_y, b)
                    wait_before(act, mm_wo, b)
                    nc.scalar.activation(yhT[:], aux[:].rearrange("p (c t) -> p c t", c=CC), ACT.Copy).then_inc(yh_ok[0], 1)

                def ffn_scaled(i):
                    wait(act, pr, b, i + 1)
                    wait(act, a2_ok, b, i + 1)
                    if i == 0:
                        wait_before(act, xa_ok, b)
                    nc.scalar.activation(ffn[:, i, :], ffn_bank(front)[:, i * C:(i + 1) * C], ACT.Copy, scale=a2[:, i:i + 1]).then_inc(ffn_ok[0], 1)

                if back and front:
                    transposed_high()
                    wait(act, pr, b)
                    ffn_scaled(0)
                    ffn_scaled(1)
                elif back:
                    wait(act, pr, b)
                    ffn_scaled(0)
                    ffn_scaled(1)
                    transposed_high()
                if back and rows:
                    n = b + 2
                    wait(act, gxq_ok, n)
                    wait(act, tr_x, f)
                    for i in range(TT_):
                        nc.scalar.activation(txs[:, i, :], cx[:, i, :], ACT.Copy, scale=gxq[:, i:i + 1]).then_inc(tx_ok[0], 1)
                if back and front:
                    wait(act, mm_wo, b)
                    wait_before(act, o_ok, b)
                    nc.scalar.activation(att[:], aux[:].rearrange("p (i c) -> p i c", i=TT_), ACT.Copy, scale=un[:, 1:2]).then_inc(att_ok[0], 1)

            def weights():
                act.wait_ge(undo, 1)
                act.wait_ge(ld_wf, 16)
                for c in range(FC):
                    nc.scalar.activation(tern[:, 0, c * C:(c + 1) * C], wfc_r[:, c, :], ACT.Abs,
                                         accum_out=wsum[:, 0, c:c + 1]).then_inc(w_abs, 1)

            def weights_transposed():
                for c, src in enumerate((acc[:], aux[:])):
                    act.wait_ge(w_tr, 4 + c)
                    nc.scalar.activation(fcT[:, c, :], src.bitcast(fp16), ACT.Copy).then_inc(w_ev, 1)
                for j, src in enumerate((acc[:], aux[:])):
                    act.wait_ge(w_tr, 6 + j)
                    nc.scalar.activation(prT[:, 4 * j:4 * j + 4, :], src.bitcast(fp16).rearrange("p (k c) -> p k c", k=4),
                                         ACT.Copy).then_inc(w_ev, 1)

            schedule(act, body)

        @block.vector
        def _(dve):
            def flat(t):
                return t.rearrange("p a n -> p (a n)")

            pro = [0]

            def did_pro(ins):
                pro[0] += 1
                ins.then_inc(dve_pro, 1)

            def settle_pro():
                dve.wait_ge(dve_pro, pro[0])

            def squared_norms():
                dve.wait_ge(w_sqtot, 1)
                nc.vector.tensor_scalar(sq[:], acc[:, 0:10].rearrange("p (a c) -> p a c", a=5)[:, :, 0], LEAST, None, ALU.max).then_inc(bounds, 1)

            def scale_factors():
                dve.wait_ge(roots, 1)
                nc.vector.tensor_scalar(sc[:], rsq[:], NORM, None, ALU.mult).then_inc(scales, 1)
                did_pro(nc.vector.tensor_scalar(rr[:, 0:1], root[:, 0:1], root[:, 2:3], 1.0 / (NORM ** 2 * HD ** 0.5), ALU.mult, ALU.mult))
                did_pro(nc.vector.tensor_scalar(rr[:, 1:2], root[:, 4:5], root[:, 3:4], NORM ** -2, ALU.mult, ALU.mult))
                settle_pro()
                nc.vector.tensor_scalar(un[:], rr[:], root[:, 1:2], 1.0 / (NORM * KV_SCALE), ALU.mult, ALU.mult).then_inc(undo, 1)

            def weight_low_halves(up):
                def low(ev, k, lo, src, hi):
                    dve.wait_ge(w_ev, ev)
                    nc.vector.scalar_tensor_tensor(out=lo, in0=src, scalar=sc[0:src.shape[0], k:k + 1], in1=hi,
                                                   op0=ALU.mult, op1=ALU.subtract).then_inc(w_lo, 1)

                if not up:
                    for d in range(2):
                        low(1, 1, wkvT[:, 1, :, d, :], ps_wkv.rearrange("p (c l) -> p c l", c=CC), wkvT[:, 0, :, d, :])
                    for c in range(CC):
                        for d in range(2):
                            low(3, 0, wqT[:, 1, c, :, d, :], ps_wq[:, c * C:(c + 1) * C].rearrange("p (h e) -> p h e", h=H), wqT[:, 0, c, :, d, :])
                else:
                    low(4, 4, woT[:, 1], ps_wo.rearrange("p (c k) -> p c k", c=CC), woT[:, 0])
                    for d in range(2):
                        low(6, 2, wkT[:, 1, :, d, :], ps_wku.rearrange("p (h e) -> p h e", h=H), wkT[:, 0, :, d, :])
                    low(6, 3, wvT[:, 1], ps_wvu, wvT[:, 0])

            def weights():
                dve.wait_ge(w_tot, 1)
                did_pro(nc.vector.tensor_reduce(out=gam[:], in_=acc[:, 0:2 * FC].rearrange("p (a c) -> p a c", a=2), axis=AX.X, op=ALU.add))
                settle_pro()
                nc.vector.tensor_scalar(gam128[:], gam[:], 1.0 / (F * C * QB), None, ALU.mult).then_inc(means, 1)
                did_pro(nc.vector.tensor_scalar(thr[:], gam[:], 1.0 / (F * C), FFN_EPS, ALU.mult, ALU.add))
                settle_pro()
                nc.vector.tensor_scalar(nthr[:], thr[:], -0.5, None, ALU.mult).then_inc(w_thr, 1)
                nc.vector.tensor_scalar(thr[:], thr[:], 0.5, None, ALU.mult).then_inc(w_thr, 1)

            def weight_sums():
                dve.wait_ge(ld_wp, 16)
                nc.vector.tensor_reduce(out=wsum[:, 1, :], in_=flat(wpr_r).rearrange("p (a k) -> p a k", k=C), axis=AX.X, op=ALU.add,
                                        apply_absolute_value=True).then_inc(w_abs, 1)

            def ternary(n):
                w = flat((wfc_r, wpr_r)[n])
                if n == 0:
                    did_pro(nc.vector.tensor_scalar(neg_t[:, n], w, nthr[:, n:n + 1], None, ALU.is_lt))
                    settle_pro()
                    dve.wait_ge(w_thr, 2)
                else:
                    dve.wait_ge(w_neg, 1)
                nc.vector.scalar_tensor_tensor(out=tern[:, n], in0=w, scalar=thr[:, n:n + 1], in1=neg_t[:, n],
                                               op0=ALU.is_gt, op1=ALU.subtract).then_inc(w_tern, 1)

            def body(b, back, front, rows):
                f = b + 1
                steps = {"f": 0, "b": 0}

                def did(ins, w):
                    steps[w] += 1
                    ins.then_inc((dve_f if w == "f" else dve_b)[0], 1)

                def settle(w, how=wait):
                    how(dve, dve_f if w == "f" else dve_b, b + 2 if w == "f" else b, steps[w])

                def maxima(r):
                    wait(dve, s1, f, r + 1)
                    src = ring[AT[("f_p1", r)] % 3]
                    if r < 2:
                        nc.vector.tensor_reduce(out=mx[:, 0, 8 * r:8 * r + 8], in_=src[:].rearrange("p a (t k) -> p (a t) k", t=NT),
                                                axis=AX.X, op=ALU.max).then_inc(red1[0], 1)
                    else:
                        gp, tp = divmod(r - 2, 2)
                        o = mx[:, 1, :].rearrange("p (g t) -> p g t", g=G)[:, 2 * gp:2 * gp + 2, 2 * tp:2 * tp + 2]
                        nc.vector.tensor_reduce(out=o, in_=src[:, :, 0:2 * (T - BLK)].rearrange("p a (t k) -> p a t k", t=2),
                                                axis=AX.X, op=ALU.max).then_inc(red1[0], 1)

                n = b + 2

                def row_stats():
                    wait(dve, ld_x, n)
                    for i in range(TT_):
                        did(nc.vector.bn_stats(st1[:, i, :], xin[:, i, :]), "f")
                    settle("f", wait_apart)
                    for i in range(TT_):
                        nc.vector.bn_aggr(mv1[:, i, :], st1[:, i, :]).then_inc(var1[0], 1)

                def row_norm():
                    wait(dve, rstd1, n)
                    wait(dve, var1, n)
                    if front:
                        wait(dve, tr_x, b + 1)
                    for i in range(TT_):
                        nc.vector.tensor_scalar(xn[:, i, :], xin[:, i, :], mv1[:, i, 0:1], rs1[:, i:i + 1],
                                                ALU.subtract, ALU.mult).then_inc(xn_ok[0], 1)
                    wait(dve, xn_ok, n)
                    for i in range(TT_):
                        did(nc.vector.bn_stats(st2[:, i, :], xn[:, i, :]), "f")
                    settle("f", wait_apart)
                    for i in range(TT_):
                        did(nc.vector.bn_aggr(mv2[:, i, :], st2[:, i, :]), "f")
                    settle("f")
                    nc.vector.tensor_scalar(nmx[:], mv2[:, :, 0], -1.0, None, ALU.mult).then_inc(nmx_ok[0], 1)

                def row_scale():
                    if back:
                        wait(dve, cx_ok, n)
                    else:
                        for i in range(TT_):
                            nc.vector.tensor_scalar(cx[:, i, :], xn[:, i, :], mv2[:, i, 0:1], None, ALU.subtract).then_inc(cx_ok[0], 1)
                        wait(dve, cx_ok, n)
                    if front:
                        wait(dve, pool_f, b + 1)
                    for i in range(TT_):
                        nc.vector.tensor_reduce(out=gx[:, i:i + 1], in_=cx[:, i, :], axis=AX.X, op=ALU.max,
                                                apply_absolute_value=True).then_inc(gx_ok[0], 1)
                    wait(dve, gx_ok, n)
                    did(nc.vector.reciprocal(gxr[:], gx[:]), "f")
                    settle("f")
                    nc.vector.tensor_scalar(gxq[:], gxr[:], QB, None, ALU.mult).then_inc(gxq_ok[0], 1)
                    if not back:
                        wait(dve, gxq_ok, n)
                        for i in range(TT_):
                            nc.vector.tensor_scalar(txs[:, i, :], cx[:, i, :], gxq[:, i:i + 1], None, ALU.mult).then_inc(tx_ok[0], 1)

                if back:
                    wait(dve, mT, b)
                    wait_before(dve, s2s, b)
                    nc.vector.tensor_copy(mov[BLK:BLK + 2 * H, :], aux[BLK:BLK + 2 * H, 0:T // 2].bitcast(bf16)).then_inc(mT_ok[0], 1)
                if not (back or front):
                    row_stats()
                    row_norm()
                    squared_norms()
                    row_scale()
                    scale_factors()
                    weight_low_halves(up=False)

                def hidden_centred(i):
                    wait(dve, gelu, b, i + 1)
                    for j in range(2):
                        did(nc.vector.bn_stats(sth[:, i, j, :], gl[:, i, 512 * j:512 * j + 512]), "b")
                    settle("b", wait_apart)
                    did(nc.vector.bn_aggr(mvh[:, i, :], flat(sth[:, i])), "b")
                    settle("b")
                    nc.vector.tensor_scalar(ch[:, i, :], gl[:, i, :], mvh[:, i, 0:1], None, ALU.subtract).then_inc(ch_ok[0], 1)

                def latents_low():
                    wait(dve, mm_lat, f)
                    wait(dve, lath_ok, f)
                    nc.vector.tensor_tensor(lat[L:P], aux[L:P, 0:T], lat[L:P], ALU.subtract).then_inc(latl_ok[0], 1)
                    nc.vector.tensor_tensor(latS[L:P], aux[L:P, 0:SINK].unsqueeze(1).to_broadcast([L, H, SINK]), latS[L:P], ALU.subtract).then_inc(latl_ok[0], 1)

                def hidden_scaled(i):
                    wait(dve, ch_ok, b, i + 1)
                    if i == 0:
                        wait_before(dve, a2_ok, b)
                    nc.vector.tensor_reduce(out=gh[:, i:i + 1], in_=ch[:, i, :], axis=AX.X, op=ALU.max,
                                            apply_absolute_value=True).then_inc(gh_ok[0], 1)
                    wait(dve, gh_ok, b, i + 1)
                    did(nc.vector.reciprocal(ghr[:, i:i + 1], gh[:, i:i + 1]), "b")
                    if i == 1 and front:
                        latents_low()
                    settle("b")
                    nc.vector.tensor_scalar(t2s[:, i, :], ch[:, i, :], ghr[:, i:i + 1], QB, ALU.mult, ALU.mult).then_inc(t2[0], 1)

                def hidden_low(i):
                    wait(dve, t2h_ok, b, i + 1)
                    nc.vector.tensor_tensor(t2l[:, i].rearrange("p k n -> p (k n)"), hidden_slot(i, front)[:].rearrange("p a n -> p (a n)"),
                                            t2h[:, i].rearrange("p k n -> p (k n)"), ALU.subtract).then_inc(t2l_ok[0], 1)

                if back:
                    hidden_centred(0)
                if front:
                    wait(dve, tr_x, f)
                    src = ring[AT[("f_tr", 0)] % 3]
                    wait(dve, xh_ok, f)
                    nc.vector.tensor_tensor(xlT[:], src[:, 0, :].rearrange("p (c t) -> p c t", c=CC), xhT[:], ALU.subtract).then_inc(xl_ok[0], 1)
                    wait(dve, th_ok, f)
                    nc.vector.tensor_tensor(tlT[:], src[:, 1, :].rearrange("p (c t) -> p c t", c=CC), thT[:], ALU.subtract).then_inc(tl_ok[0], 1)
                if front and not back:
                    weight_low_halves(up=True)
                if back:
                    hidden_scaled(0)
                if rows and (front or back):
                    row_stats()
                if front and not back:
                    weight_sums()
                if back:
                    hidden_centred(1)
                    hidden_scaled(1)
                if front and not back:
                    latents_low()
                if rows and (front or back):
                    row_norm()
                if front and not back:
                    weights()
                if front:
                    wait(dve, qh_ok, f)
                    if not back:
                        dve.wait_ge(ld_const, N_CONST)
                        dve.wait_ge(memsets, N_SET)
                    nc.vector.scalar_tensor_tensor(out=flat(Q), in0=qh[:], scalar=rowlo[:, 0:1],
                                                   in1=ring[AT[("f_q", 0)] % 3][:].rearrange("p a n -> p (a n)"),
                                                   op0=ALU.mult, op1=ALU.add).then_inc(q_ok[0], 1)
                    wait(dve, kh_ok, f)
                    nc.vector.scalar_tensor_tensor(out=flat(KL), in0=ring[AT[("f_k", 0)] % 3][:].rearrange("p a n -> p (a n)"), scalar=KV_SCALE,
                                                   in1=flat(KH), op0=ALU.mult, op1=ALU.subtract).then_inc(kl_ok[0], 1)
                    wait(dve, kl_ok, f)
                    for d, s in ((BDH, KH), (BDL, KL)):
                        o = flat(d).rearrange("p (t n) -> p t n", t=NT)
                        o = bass.AP(o.tensor, o.offset, [o.ap[0], [P + SINK, NT], [NT * SINK, G], [1, SINK]])
                        nc.vector.tensor_tensor(o, s[:, :, 0:SINK].unsqueeze(2).to_broadcast([P, NT, G, SINK]),
                                                gmask[:].unsqueeze(1).unsqueeze(3).to_broadcast([P, NT, G, SINK]), ALU.mult).then_inc(bd_ok[0], 1)
                    if not back:
                        ternary(0)
                if back:
                    hidden_low(0)
                if back and not front:
                    hidden_low(1)
                if back:
                    for i in range(TT_):
                        wait(dve, pv, b, i + 1)
                        o = (acc if i == 0 else aux)[:, 0:H * VW].rearrange("p (h d) -> p h d", h=H)
                        did(nc.vector.reciprocal(rden[:, i, :], o[:, :, HD]), "b")
                        settle("b")
                        if i == 0:
                            wait_before(dve, tr_y, b)
                        nc.vector.tensor_tensor(y[:, i, :].rearrange("p (h d) -> p h d", h=H), o[:, :, 0:HD],
                                                rden[:, i, :].unsqueeze(2).to_broadcast([P, H, HD]), ALU.mult).then_inc(y_ok[0], 1)
                if back and front:
                    hidden_low(1)
                if front:
                    wait(dve, vh_ok, f)
                    nc.vector.scalar_tensor_tensor(out=VL[:, :, :, 0:HD], in0=ring[AT[("f_v", 0)] % 3][:].rearrange("p a n -> p (a n)")[:, 0:3 * C]
                                                   .rearrange("p (j h d) -> p j h d", j=3, h=H), scalar=KV_SCALE, in1=VH[:, :, :, 0:HD],
                                                   op0=ALU.mult, op1=ALU.subtract).then_inc(v_ok[0], 1)
                    wait(dve, mm_v, f)
                    nc.vector.scalar_tensor_tensor(out=vs32[:], in0=ring[AT[("f_v", 0)] % 3][0:H * SINK, 1, C:2 * C].rearrange("p (h d) -> p h d", h=H), scalar=KV_SCALE,
                                                   in1=vsmask[:].unsqueeze(2).to_broadcast([H * SINK, H, HD]), op0=ALU.mult, op1=ALU.mult).then_inc(vs_ok[0], 1)
                if back:
                    wait(dve, yh_ok, b)
                    wait_before(dve, mm_wo, b)
                    nc.vector.tensor_tensor(ylT[:], aux[:].rearrange("p (c t) -> p c t", c=CC), yhT[:], ALU.subtract).then_inc(yl_ok[0], 1)
                if rows and back:
                    row_scale()
                if front:
                    for r in range(6):
                        if not back and r == 3:
                            ternary(1)
                        if not back and r == 5:
                            row_scale()
                        maxima(r)
                    nc.vector.tensor_reduce(out=flat(smx), in_=ring[AT[("f_p1", 5)] % 3][:, 0, 512 - TT_ * H * SINK:512].rearrange("p (h s) -> p h s", s=SINK),
                                            axis=AX.X, op=ALU.max).then_inc(red1s[0], 1)
                    wait(dve, red1, f)
                    wait(dve, red1s, f)
                    nc.vector.tensor_tensor(flat(mm), flat(mx), flat(smx), ALU.max).then_inc(mm_ok[0], 1)
                    wait(dve, mm_ok, f)
                    if back:
                        wait(dve, mT, b)
                    nc.vector.tensor_scalar(mhl[:, :, 0, :], mm[:], -1.0, None, ALU.mult).then_inc(m_ok[0], 1)
                    wait(dve, m_ok, f, 1)
                    nc.vector.scalar_tensor_tensor(out=mhl[:, :, 1, :], in0=mm[:], scalar=-1.0, in1=mhl[:, :, 0, :],
                                                   op0=ALU.mult, op1=ALU.subtract).then_inc(m_ok[0], 1)
                if back and not front:
                    wait(dve, mm_wo, b)
                    wait(dve, xa_ok, b)
                    wait_before(dve, st_out, b)
                    nc.vector.scalar_tensor_tensor(out=ob[:], in0=aux[:].rearrange("p (i c) -> p i c", i=TT_), scalar=un[:, 1:2],
                                                   in1=xff[:], op0=ALU.mult, op1=ALU.add).then_inc(o_ok[0], 1)
                assert not rows or steps["f"] == DF, steps
                assert not back or steps["b"] == DB, steps

            schedule(dve, body)

        @block.tensor
        def _(pe):
            def flat(t):
                return t.rearrange("p a n -> p (a n)")

            pe.wait_ge(ld_id, 16)
            pe.wait_ge(ld_w[0], 16)
            for c in range(CC):
                for r in range(CC):
                    last = nc.tensor.transpose(ps_wq[:, c * C + r * P:c * C + (r + 1) * P], wq_r[:, r, c * P:(c + 1) * P], idf[:])
            last.then_inc(w_tr, 1)
            pe.wait_ge(ld_w[1], 16)
            for c in range(CC):
                nc.tensor.transpose(ps_wkv[:, c * L:(c + 1) * L], wkv_r[:, c * P:(c + 1) * P], idf[0:L, 0:L])
            for n, (w, dst) in enumerate(((wku_r, ps_wku), (wvu_r, ps_wvu))):
                pe.wait_ge(ld_w[2 + n], 32)
                for r in range(CC):
                    last = nc.tensor.transpose(dst[:, r * P:(r + 1) * P], w[:, r].rearrange("p d l -> p (d l)"), idf[:])
            last.then_inc(w_tr, 1)
            pe.wait_ge(ld_w[4], 16)
            for c in range(CC):
                for r in range(CC):
                    last = nc.tensor.transpose(ps_wo[:, c * C + r * P:c * C + (r + 1) * P], wo_r[:, r, c * P:(c + 1) * P], idf[:])
            last.then_inc(w_tr, 1)
            pe.wait_ge(w_sq, 5)
            nc.tensor.matmul(acc[:, 0:10], ones[:], flat(wsq), start=True, stop=True).then_inc(w_sqtot, 1)
            N_EV, N_LO = 6, 10
            HALVES = ((0, 0), (0, 1), (1, 0))
            STACKED = ((0, P), (1, L))

            def weight_totals():
                pe.wait_ge(w_abs, FC + 1)
                pe.wait_ge(bounds, 1)
                nc.tensor.matmul(acc[:, 0:2 * FC], ones[:], flat(wsum), start=True, stop=True).then_inc(w_tot, 1)

            def first_ternary():
                pe.wait_ge(w_tern, 1)
                pe.wait_ge(means, 1)
                wait(pe, latl_ok, 0)
                for c, dst in enumerate((acc[:], aux[:])):
                    for k in range(FC):
                        last = nc.tensor.transpose(dst.bitcast(fp16)[:, k * P:(k + 1) * P],
                                                   tern[:, 0, k * C + c * P:k * C + (c + 1) * P], idh[:])
                    last.then_inc(w_tr, 1)

            def second_ternary():
                pe.wait_ge(w_tern, 2)
                for j, dst in enumerate((acc[:], aux[:])):
                    pe.wait_ge(w_ev, N_EV + 1 + j)
                    for k in range(4):
                        for c in range(CC):
                            last = nc.tensor.transpose(dst.bitcast(fp16)[:, k * C + c * P:k * C + (c + 1) * P],
                                                       tern[:, 1, c * F + (4 * j + k) * P:c * F + (4 * j + k + 1) * P], idh[:])
                    last.then_inc(w_tr, 1)

            def body(b, back, front, rows):
                f = b + 1

                def slot(name, i=0):
                    return take(pe, name, i, b, back, front)

                def fc_tile(i):
                    if i == 0:
                        wait(pe, th_ok, b); wait(pe, tl_ok, b)
                    s = slot("fc", i)
                    for n in range(2):
                        for m, (c, src) in enumerate([(c, src) for src in (thT, tlT) for c in range(CC)]):
                            last = nc.tensor.matmul(s[:, n, :], src[:, c, i * P:(i + 1) * P], fcT[:, c, 512 * n:512 * n + 512],
                                                    start=(m == 0), stop=(m == 2 * CC - 1))
                    last.then_inc(fc[0], 1)

                def sink_scores(o):
                    wait(pe, bd_ok, f)
                    nc.tensor.matmul(o[:, 0:H * SINK], idb[:], msink[:], start=True, stop=False, skip_group_check=True)
                    for i in range(TT_):
                        for t in range(NT):
                            last = nc.tensor.matmul(o[:, i * H * SINK:(i + 1) * H * SINK], Q[:, t, i * P:(i + 1) * P], BDH[:, t, 0:H * SINK],
                                                    start=False, stop=(t == NT - 1), skip_group_check=True)
                    return last

                def window_scores(r):
                    if r == 0:
                        if not back:
                            pe.wait_ge(ld_const, N_CONST)
                        wait(pe, q_ok, f)
                        wait(pe, kh_ok, f)
                    s = slot("f_p1", r)
                    q0, k0, heads, mask = (0, 0, range(NT), mask0) if r < 2 else (P, BLK, range(2 * (r % 2), 2 * (r % 2) + 2), mask1)
                    n, gp = mask.shape[1], (r if r < 2 else (r - 2) // 2)
                    for a in range(2):
                        nc.tensor.matmul(s[:, a, 0:n * len(heads)].rearrange("p (t k) -> p t k", t=len(heads)), idb[:],
                                         mask[:].unsqueeze(1).to_broadcast([P, len(heads), n]), start=True, stop=False, skip_group_check=True)
                    for j, t in enumerate(heads):
                        for a in range(2):
                            g = 32 * (2 * gp + a)
                            last = nc.tensor.matmul(s[:, a, n * j:n * j + n], Q[g:g + 32, t, q0:q0 + P], KH[g:g + 32, t, k0:k0 + n],
                                                    start=False, stop=True, skip_group_check=True)
                    if r == 5:
                        last = sink_scores(s[:, 0, 512 - TT_ * H * SINK:512])
                    last.then_inc(s1[0], 1)

                def transposed_rows():
                    s = slot("f_tr")
                    wait(pe, xn_ok, f)
                    for c in range(CC):
                        for i in range(TT_):
                            nc.tensor.transpose(s[:, 0, c * T + i * P:c * T + (i + 1) * P], xn[:, i, c * P:(c + 1) * P], idf[:])
                    wait(pe, tx_ok, f)
                    for c in range(CC):
                        for i in range(TT_):
                            last = nc.tensor.transpose(s[:, 1, c * T + i * P:c * T + (i + 1) * P], txs[:, i, c * P:(c + 1) * P], idf[:])
                    last.then_inc(tr_x[0], 1)

                def latents():
                    wait(pe, xh_ok, f)
                    wait(pe, xl_ok, f)
                    if not back:
                        pe.wait_ge(w_lo, 2)
                    if back:
                        wait(pe, exs, b)
                    for n, (x_half, w_half) in enumerate(HALVES):
                        for c in range(CC):
                            last = nc.tensor.matmul(aux[:, 0:T], wkvT[:, w_half, c].rearrange("p d l -> p (d l)"), (xhT, xlT)[x_half][:, c, :],
                                                    start=(n == 0 and c == 0), stop=(n == 2 and c == CC - 1))
                    last.then_inc(mm_lat[0], 1)

                if back:
                    fc_tile(0)
                    fc_tile(1)
                    wait(pe, m_ok, b)
                    wait_before(pe, att_ok, b)
                    for i in range(TT_):
                        last = nc.tensor.transpose(aux[BLK:BLK + 2 * H, 0:T // 2].bitcast(bf16)[:, i * P:(i + 1) * P],
                                                   mhl[:, i].rearrange("p a h -> p (a h)"), idb[:])
                    last.then_inc(mT[0], 1)
                    if front:
                        transposed_rows()
                    wait(pe, mT_ok, b); wait(pe, kl_ok, b)
                    nc.tensor.matmul(aux[:, 0:T], bias[:, 2 * H, :], mov[:], start=True, stop=False, skip_group_check=True)
                    for t in range(NT):
                        for K in (BDH, BDL):
                            last = nc.tensor.matmul(aux[:, 0:T], K[:, t, :], Q[:, t, :], start=False,
                                                    stop=(t == NT - 1 and K is BDL), skip_group_check=True)
                    last.then_inc(s2s[0], 1)
                    for r in range(4):
                        gp, tp = divmod(r, 2)
                        s = slot("p2", r)
                        for j in range(2):
                            for a in range(2):
                                hm = NT * (2 * gp + a) + 2 * tp + j
                                nc.tensor.matmul(s[:, a, T * j:T * j + BLK], bias[:, hm, :], mov[:, 0:BLK],
                                                 start=(j == 0), stop=False, skip_group_check=True)
                                nc.tensor.matmul(s[:, a, T * j + BLK:T * j + T], bias[:, H + hm, :], mov[:, BLK:T],
                                                 start=False, stop=False, skip_group_check=True)
                        for j in range(2):
                            t = 2 * tp + j
                            for q0, n, k0 in ((0, P, 0), (P, BLK, BLK), (P + BLK, BLK, P)):
                                for K in (KH, KL):
                                    for a in range(2):
                                        g = 32 * (2 * gp + a)
                                        last = nc.tensor.matmul(s[:, a, T * j + q0:T * j + q0 + n], K[g:g + 32, t, k0:k0 + P],
                                                                Q[g:g + 32, t, q0:q0 + n], start=False, stop=True, skip_group_check=True)
                        last.then_inc(s2[0], 1)
                        if front and r == 2:
                            latents()
                if front:
                    if not back:
                        transposed_rows()
                        latents()

                def q_products():
                    if not back:
                        pe.wait_ge(w_lo, 7)
                    s = slot("f_q")
                    for t in range(NT):
                        for n, (x_half, w_half) in enumerate(HALVES):
                            for c in range(CC):
                                last = nc.tensor.matmul(s[:, t // 2, (t % 2) * T:(t % 2 + 1) * T],
                                                        wqT[:, w_half, c, G * t:G * t + G].rearrange("p h d e -> p (h d e)"), (xhT, xlT)[x_half][:, c, :],
                                                        start=(n == 0 and c == 0), stop=(n == 2 and c == CC - 1), skip_group_check=True)
                    last.then_inc(mm_q[0], 1)

                def k_products():
                    wait(pe, lath_ok, f)
                    wait(pe, latl_ok, f)
                    if not back:
                        pe.wait_ge(w_lo, N_LO)
                    s = slot("f_k")
                    for t in range(NT):
                        for w_half, rows_ in STACKED:
                            last = nc.tensor.matmul(s[:, t // 2, (t % 2) * T:(t % 2 + 1) * T],
                                                    wkT[0:rows_, w_half, G * t:G * t + G].rearrange("p h d e -> p (h d e)"), lat[0:rows_],
                                                    start=(w_half == 0), stop=(w_half == 1), skip_group_check=True)
                    last.then_inc(mm_k[0], 1)

                def hidden_transposed(i):
                    wait(pe, t2, b, i + 1)
                    if front:
                        slot("t2T", i)
                    else:
                        wait(pe, exh, b, 2 + i)
                    s = hidden_slot(i, front)
                    for k in range(FC):
                        last = nc.tensor.transpose(s[:, k // 4, (k % 4) * P:(k % 4 + 1) * P], t2s[:, i, k * P:(k + 1) * P], idf[:])
                    last.then_inc(tr_h[0], 1)

                def second_product(i):
                    wait(pe, t2h_ok, b, i + 1)
                    wait(pe, t2l_ok, b, i + 1)
                    o = ffn_bank(front)
                    if not front:
                        wait(pe, exh, b)
                    for k in range(FC):
                        for src in (t2h, t2l):
                            last = nc.tensor.matmul(o[:, i * C:(i + 1) * C], src[:, i, k, :], prT[:, k, :],
                                                    start=(k == 0 and src is t2h), stop=(k == FC - 1 and src is t2l), skip_group_check=True)
                    last.then_inc(pr[0], 1)

                def values(probs, probs_sink, parts_v, first, rounds=range(4)):
                    for i, o in ((0, acc), (1, aux)):
                        for n, (_, vsink) in enumerate(parts_v if 0 in rounds else ()):
                            nc.tensor.matmul(o[:, 0:H * VW], probs_sink[:, i * P:(i + 1) * P], vsink[:].rearrange("p h d -> p (h d)"),
                                             start=(first and n == 0), stop=False, skip_group_check=True)
                        for h in range(H):
                            t, g = divmod(h, G)
                            if 2 * (g // 2) + t // 2 not in rounds:
                                continue
                            parts = ((0, P, 0, 0),) if i == 0 else ((0, BLK, P, 1), (BLK, BLK, P + BLK, 2))
                            for p0, m, q0, v in parts:
                                for w, _ in parts_v:
                                    last = nc.tensor.matmul(o[p0:p0 + m, h * VW:(h + 1) * VW], probs[:, g, t, q0:q0 + m], w[:, v, h, :],
                                                            start=False, stop=not first, skip_group_check=True)
                        if not first:
                            last.then_inc(pv[0], 1)

                if front:
                    q_products()
                    k_products()
                    if not back:
                        weight_totals()
                if back:
                    if front:
                        hidden_transposed(0)
                    wait(pe, vs_ok, b)
                    wait(pe, exs, b)
                    wait_before(pe, ffn_ok, b)
                    if front:
                        wait(pe, exh, b)
                        wait(pe, latl_ok, f)
                        values(EH, ESH, ((VH, VSH), (VL, VSL)), True)
                        hidden_transposed(1)
                    else:
                        for r in range(4):
                            wait(pe, exh, b, r + 1)
                            values(EH, ESH, ((VH, VSH), (VL, VSL)), True, (r,))
                            if r in (1, 2):
                                hidden_transposed(r - 1)
                        second_product(0)
                        second_product(1)
                    wait(pe, els, b)
                    wait(pe, el_ok, b)
                    values(EL, ESL, ((VH, VSH),), False)
                if front:
                    s = slot("f_v")
                    for j in range(3):
                        for w_half, rows_ in STACKED:
                            last = nc.tensor.matmul(s[:, j // 2, (j % 2) * C:(j % 2 + 1) * C], lat[0:rows_, BLK * j:BLK * j + P],
                                                    wvT[0:rows_, w_half], start=(w_half == 0), stop=(w_half == 1), skip_group_check=True)
                    for w_half, rows_ in STACKED:
                        last = nc.tensor.matmul(s[0:H * SINK, 1, C:2 * C], latS[0:rows_].rearrange("p h s -> p (h s)"), wvT[0:rows_, w_half],
                                                start=(w_half == 0), stop=(w_half == 1), skip_group_check=True)
                    last.then_inc(mm_v[0], 1)
                if back:
                    wait(pe, y_ok, b)
                    for c in range(CC):
                        for i in range(TT_):
                            last = nc.tensor.transpose(aux[:, c * T + i * P:c * T + (i + 1) * P], y[:, i, c * P:(c + 1) * P], idf[:])
                    last.then_inc(tr_y[0], 1)
                for i in range(TT_):
                    if back and front:
                        second_product(i)
                    if i == 1 and back:
                        wait(pe, yh_ok, b)
                        wait(pe, yl_ok, b)
                        for j in range(TT_):
                            for n, (y_half, w_half) in enumerate(HALVES):
                                for c in range(CC):
                                    last = nc.tensor.matmul(aux[:, j * C:(j + 1) * C], (yhT, ylT)[y_half][:, c, j * P:(j + 1) * P], woT[:, w_half, c, :],
                                                            start=(n == 0 and c == 0), stop=(n == 2 and c == CC - 1), skip_group_check=True)
                        last.then_inc(mm_wo[0], 1)
                    if front:
                        for r in range(3 * i, 3 * i + 3):
                            window_scores(r)
                            if not back and r == 2:
                                first_ternary()
                            if not back and r == 4:
                                second_ternary()
                if front and not back:
                    pe.wait_ge(w_ev, N_EV + 4)

            schedule(pe, body)


def shape_constants():
    import numpy as np

    def bf16_bits(a):
        return (np.ascontiguousarray(a, np.float32).view(np.uint32) >> 16).astype(np.uint16)

    k = {}
    k["c_idf"] = np.eye(P, dtype=np.float32)
    k["c_idh"] = np.eye(P, dtype=np.float16)
    k["c_idb"] = bf16_bits(np.eye(P))
    q, j = np.arange(T)[:, None], np.arange(T)[None, :]
    band = (j <= q) & (j >= q - (WINDOW - 1))
    mask = np.where(band, 0.0, MASKED)
    k["c_mask0"] = bf16_bits(mask[0:P, 0:P])
    k["c_mask1"] = bf16_bits(mask[P:T, BLK:T])
    sink = np.where(np.arange(SINK)[None, :] <= q - WINDOW, 0.0, MASKED)
    k["c_msink"] = bf16_bits(np.tile(sink[0:P], (1, H)))
    bias = np.zeros((BIAS_ROWS, 2 * H + 1, P), np.float32)
    for hm in range(H):
        bias[0:BLK, hm] = mask[0:BLK, 0:P]
        bias[0:BLK, H + hm] = mask[BLK:P, 0:P]
        for n in (hm, H + hm):
            bias[BLK + hm, n] = bias[BLK + H + hm, n] = 1.0
        bias[BLK + hm, 2 * H, hm * SINK:(hm + 1) * SINK] = 1.0
        bias[BLK + H + hm, 2 * H, hm * SINK:(hm + 1) * SINK] = 1.0
        for s in range(SINK):
            bias[BLK + 2 * H + s, 2 * H, hm * SINK + s] = MASKED
    k["c_bias"] = bf16_bits(bias)
    mov = np.zeros((BIAS_ROWS, T), np.float32)
    mov[0:BLK] = np.tile(np.eye(BLK), (1, T // BLK))
    mov[BLK + 2 * H:] = (sink != 0).T
    k["c_mov"] = bf16_bits(mov)
    p = np.arange(P)
    k["c_rowlo"] = -((p % 32) >= HD).astype(np.float32)[:, None]
    k["c_gmask"] = (p[:, None] // 32 == np.arange(G)[None, :]).astype(np.float32)
    hm = np.arange(H * SINK) // SINK
    own = ((hm % NT) * G + hm // NT)[:, None] == np.arange(H)[None, :]
    k["c_vsmask"] = own.astype(np.float32)
    k["c_vsones"] = np.zeros((H * SINK, H, VW), np.float16)
    k["c_vsones"][:, :, HD] = own
    return k


_INS = ["L0_attn_x", "L0_attn_Wq", "L0_attn_Wkv_down", "L0_attn_Wk_up", "L0_attn_Wv_up", "L0_attn_Wo",
        "L0_ffn_w_fc", "L0_ffn_w_proj"]


def kernel(**inputs):
    import numpy as np
    import concourse.bacc as bacc
    from concourse.bass_utils import run_bass_kernel_spmd

    nc = bacc.Bacc("TRN2", target_bir_lowering=False, num_devices=1)
    arrays, args = {}, []
    given = {name: np.ascontiguousarray(inputs[name]) for name in _INS}
    for name, a in {**given, **shape_constants()}.items():
        arrays[f"in_{name}"] = a
        args.append(nc.dram_tensor(f"in_{name}", a.shape, mybir.dt.from_np(a.dtype), kind="ExternalInput").ap())
    args.append(nc.dram_tensor("out_0", (B, T, C), mybir.dt.float32, kind="ExternalOutput").ap())
    layer_kernel(nc, *args)
    r = run_bass_kernel_spmd(nc, [arrays], core_ids=[0])
    return r.results[0]["out_0"]
```
